# Optimizing a Trainium2 kernel written in Bass

```python
import numpy as np
import jax
import jax.numpy as jnp

def _softmax(x, axis=-1):
    return jax.nn.softmax(x, axis=axis)

def _gelu(x):
    return jax.nn.gelu(x, approximate=True)

def _silu(x):
    return jax.nn.silu(x)

def _sigmoid(x):
    return jax.nn.sigmoid(x)

def _layernorm(x, axis=-1, eps=1e-05):
    m = jnp.mean(x, axis=axis, keepdims=True)
    v = jnp.var(x, axis=axis, keepdims=True)
    return (x - m) / jnp.sqrt(v + eps)

def _scatter_add(tgt, idx, src, axis=0):
    return tgt.at[idx].add(src)

def _segment_sum(src, seg, n):
    return jax.ops.segment_sum(src, seg, n)
kernel_name = 'mk_cond_resid_d4_seqx_r8_0b40dd'

def setup_inputs(seed: int=0):
    np.random.seed(seed)
    _w = jnp.asarray

    def _rec_inputs():
        import jax
        import jax.numpy as jnp
        _rk = jax.random.key(seed)
        x = -0.000125 + 0.9999 * jax.random.normal(jax.random.fold_in(_rk, 1), (64, 32, 256), jnp.float32)
        _lenS = 32 - jax.random.randint(jax.random.fold_in(_rk, 7), (64,), 0, max(1, 32 // 4) + 1, jnp.int32)
        _lenS2 = 32 - jax.random.randint(jax.random.fold_in(_rk, 8), (64,), 0, max(1, 32 // 4) + 1, jnp.int32)
        itok_B_0_7 = jax.random.randint(jax.random.fold_in(_rk, 11), (64,), 0, 8, jnp.int32)
        fside_8xS_0 = -0.00162727 + 0.0609077 * jax.random.normal(jax.random.fold_in(_rk, 12), (8, 32), jnp.float32)
        itok_Bx257_0_4111 = jax.random.randint(jax.random.fold_in(_rk, 13), (64, 257), 0, 514, jnp.int32)
        itok_B_37_3939 = jax.random.randint(jax.random.fold_in(_rk, 14), (64,), 37, 3940, jnp.int32)
        return (x, itok_B_0_7, fside_8xS_0, itok_Bx257_0_4111, itok_B_37_3939)
    x, itok_B_0_7, fside_8xS_0, itok_Bx257_0_4111, itok_B_37_3939 = _rec_inputs()

    def _L0_cond_setup():
        import jax, jax.numpy as jnp
        import numpy as np
        B, C, T = (64, 32, 256)
        D, N = (32, 8)
        key = jax.random.key(seed)
        k_x, k_s, k_w, k_b = jax.random.split(key, 4)
        scale = 1.0 / np.sqrt(C)
        x = jax.random.normal(k_x, (B, C, T), dtype=jnp.float32)
        subjects = jax.random.randint(k_s, (B,), 0, N, dtype=jnp.int64)
        weights = jax.random.normal(k_w, (N, C, D), dtype=jnp.float32) * scale
        bias = jax.random.normal(k_b, (N, D), dtype=jnp.float32) * scale
        return {'x': x, 'subjects': subjects, 'weights': weights, 'bias': bias}
    _L0_cond_all = _L0_cond_setup()
    _L0_cond_in = {k: v for k, v in _L0_cond_all.items() if k in ('weights',)}
    del _L0_cond_all

    def _L1_cond_setup():
        import jax, jax.numpy as jnp
        import numpy as np
        B, C, D, T, N_SUBJECTS = (128, 32, 32, 256, 8)
        key = jax.random.key(seed)
        kx, ks, kw = jax.random.split(key, 3)
        x = jax.random.normal(kx, (B, C, T), dtype=jnp.float32)
        subjects = jax.random.randint(ks, (B,), 0, N_SUBJECTS, dtype=jnp.int64)
        weights = jax.random.normal(kw, (N_SUBJECTS, C, D), dtype=jnp.float32) * (1.0 / C ** 0.5)
        return {'x': x, 'subjects': subjects, 'weights': weights}
    _L1_cond_all = _L1_cond_setup()
    _L1_cond_in = {k: v for k, v in _L1_cond_all.items() if k in ('weights',)}
    del _L1_cond_all

    def _L2_cond_setup():
        import jax, jax.numpy as jnp
        import numpy as np
        H, G, HD = (8, 4, 32)
        GSZ = H // G
        BLOCK = 16
        WINDOW = 128
        SCALE = 256.0 ** (-0.5)
        EPS = 1e-06
        THETA = 10000.0
        B, T, D = (16, 4, 256)
        NBLK = 257

        def _rms(x, scale):
            var = jnp.mean(x * x, axis=-1, keepdims=True)
            return x * jax.lax.rsqrt(var + EPS) * (1.0 + scale)

        def _rope(x, pos):
            half = HD // 2
            inv = 1.0 / THETA ** (jnp.arange(half, dtype=jnp.float32) / half)
            ang = pos[:, :, None].astype(jnp.float32) * inv
            cos = jnp.cos(ang)[:, None, :, :]
            sin = jnp.sin(ang)[:, None, :, :]
            x1, x2 = (x[..., :half], x[..., half:])
            return jnp.concatenate([x1 * cos - x2 * sin, x2 * cos + x1 * sin], axis=-1)
        key = jax.random.key(seed)
        ks = jax.random.split(key, 10)
        inv_d = 1.0 / np.sqrt(D)
        return {'x': jax.random.normal(ks[0], (B, T, D), jnp.float32), 'Wq': jax.random.normal(ks[1], (H * HD, D), jnp.float32) * inv_d, 'Wk': jax.random.normal(ks[2], (G * HD, D), jnp.float32) * inv_d, 'Wv': jax.random.normal(ks[3], (G * HD, D), jnp.float32) * inv_d, 'Wo': jax.random.normal(ks[4], (D, H * HD), jnp.float32) * inv_d, 'q_norm_scale': jax.random.normal(ks[5], (HD,), jnp.float32) * 0.02, 'k_norm_scale': jax.random.normal(ks[6], (HD,), jnp.float32) * 0.02, 'k_blocks': jax.random.normal(ks[7], (B * NBLK, G, BLOCK, HD), jnp.float32), 'v_blocks': jax.random.normal(ks[8], (B * NBLK, G, BLOCK, HD), jnp.float32), 'block_tables': jnp.arange(B * NBLK, dtype=jnp.int32).reshape(B, NBLK), 'kv_lens': jax.random.randint(ks[9], (B,), 0, 512, dtype=jnp.int32)}
    _L2_cond_all = _L2_cond_setup()
    _L2_cond_in = {k: v for k, v in _L2_cond_all.items() if k in ('Wq', 'Wk', 'Wv', 'Wo', 'q_norm_scale', 'k_norm_scale', 'k_blocks', 'v_blocks')}
    del _L2_cond_all

    def _L3_cond_setup():
        import jax, jax.numpy as jnp
        import numpy as np

        def _lora_linear(x, W, A, B, adapter_indices):
            base = jnp.einsum('bsd,df->bsf', x, W)
            Ai = A[adapter_indices]
            Bi = B[adapter_indices]
            lora = jnp.einsum('bsr,brf->bsf', jnp.einsum('bsd,bdr->bsr', x, Ai), Bi)
            return base + lora
        key = jax.random.key(seed)
        ks = jax.random.split(key, 10)
        H, I, N, R = (256, 1024, 8, 16)
        B, S = (4, 256)
        std_h = 1.0 / np.sqrt(H)
        std_i = 1.0 / np.sqrt(I)
        x = jax.random.normal(ks[0], (B, S, H), dtype=jnp.float32)
        adapter_indices = jax.random.randint(ks[1], (B,), 0, N, dtype=jnp.int32)
        Wg = jax.random.normal(ks[2], (H, I), dtype=jnp.float32) * std_h
        Wu = jax.random.normal(ks[3], (H, I), dtype=jnp.float32) * std_h
        Wd = jax.random.normal(ks[4], (I, H), dtype=jnp.float32) * std_i
        Ag = jax.random.normal(ks[5], (N, H, R), dtype=jnp.float32) * std_h
        Bg = jnp.zeros((N, R, I), dtype=jnp.float32) + 0.01
        Au = jax.random.normal(ks[6], (N, H, R), dtype=jnp.float32) * std_h
        Bu = jnp.zeros((N, R, I), dtype=jnp.float32) + 0.01
        Ad = jax.random.normal(ks[7], (N, I, R), dtype=jnp.float32) * std_i
        Bd = jnp.zeros((N, R, H), dtype=jnp.float32) + 0.01
        return {'x': x, 'Wg': Wg, 'Wu': Wu, 'Wd': Wd, 'Ag': Ag, 'Bg': Bg, 'Au': Au, 'Bu': Bu, 'Ad': Ad, 'Bd': Bd, 'adapter_indices': adapter_indices}
    _L3_cond_all = _L3_cond_setup()
    _L3_cond_in = {k: v for k, v in _L3_cond_all.items() if k in ('Wg', 'Wu', 'Wd', 'Ag', 'Bg', 'Au', 'Bu', 'Ad', 'Bd')}
    del _L3_cond_all
    return {'x': x, 'itok_B_0_7': itok_B_0_7, 'fside_8xS_0': fside_8xS_0, 'itok_Bx257_0_4111': itok_Bx257_0_4111, 'itok_B_37_3939': itok_B_37_3939, 'L0_cond_weights': _L0_cond_in['weights'], 'L1_cond_weights': _L1_cond_in['weights'], 'L2_cond_Wq': _L2_cond_in['Wq'], 'L2_cond_Wk': _L2_cond_in['Wk'], 'L2_cond_Wv': _L2_cond_in['Wv'], 'L2_cond_Wo': _L2_cond_in['Wo'], 'L2_cond_q_norm_scale': _L2_cond_in['q_norm_scale'], 'L2_cond_k_norm_scale': _L2_cond_in['k_norm_scale'], 'L2_cond_k_blocks': _L2_cond_in['k_blocks'], 'L2_cond_v_blocks': _L2_cond_in['v_blocks'], 'L3_cond_Wg': _L3_cond_in['Wg'], 'L3_cond_Wu': _L3_cond_in['Wu'], 'L3_cond_Wd': _L3_cond_in['Wd'], 'L3_cond_Ag': _L3_cond_in['Ag'], 'L3_cond_Bg': _L3_cond_in['Bg'], 'L3_cond_Au': _L3_cond_in['Au'], 'L3_cond_Bu': _L3_cond_in['Bu'], 'L3_cond_Ad': _L3_cond_in['Ad'], 'L3_cond_Bd': _L3_cond_in['Bd']}

def reference(x, itok_B_0_7, fside_8xS_0, itok_Bx257_0_4111, itok_B_37_3939, L0_cond_weights, L1_cond_weights, L2_cond_Wq, L2_cond_Wk, L2_cond_Wv, L2_cond_Wo, L2_cond_q_norm_scale, L2_cond_k_norm_scale, L2_cond_k_blocks, L2_cond_v_blocks, L3_cond_Wg, L3_cond_Wu, L3_cond_Wd, L3_cond_Ag, L3_cond_Bg, L3_cond_Au, L3_cond_Bu, L3_cond_Ad, L3_cond_Bd):
    import jax
    import jax.numpy as jnp

    def _L0_cond_ref(x, subjects, weights, bias):
        import jax, jax.numpy as jnp
        import numpy as np
        B, C, T = (64, 32, 256)
        D, N = (32, 8)
        w = weights[subjects]
        b = bias[subjects]
        out = jnp.einsum('bct,bcd->bdt', x, w)
        out = out + b[:, :, None]
        return out

    def _L1_cond_ref(x, subjects, weights):
        import jax, jax.numpy as jnp
        import numpy as np
        B, C, D, T, N_SUBJECTS = (128, 32, 32, 256, 8)
        w = weights[subjects]
        out = jnp.einsum('bct,bcd->bdt', x, w)
        return out

    def _L2_cond_ref(x, Wq, Wk, Wv, Wo, q_norm_scale, k_norm_scale, k_blocks, v_blocks, block_tables, kv_lens):
        import jax, jax.numpy as jnp
        import numpy as np
        H, G, HD = (8, 4, 32)
        GSZ = H // G
        BLOCK = 16
        WINDOW = 128
        SCALE = 256.0 ** (-0.5)
        EPS = 1e-06
        THETA = 10000.0
        B, T, D = (16, 4, 256)
        NBLK = 257

        def _rms(x, scale):
            var = jnp.mean(x * x, axis=-1, keepdims=True)
            return x * jax.lax.rsqrt(var + EPS) * (1.0 + scale)

        def _rope(x, pos):
            half = HD // 2
            inv = 1.0 / THETA ** (jnp.arange(half, dtype=jnp.float32) / half)
            ang = pos[:, :, None].astype(jnp.float32) * inv
            cos = jnp.cos(ang)[:, None, :, :]
            sin = jnp.sin(ang)[:, None, :, :]
            x1, x2 = (x[..., :half], x[..., half:])
            return jnp.concatenate([x1 * cos - x2 * sin, x2 * cos + x1 * sin], axis=-1)
        Bx, Tx, _ = x.shape
        q = jnp.einsum('btd,od->bto', x, Wq).reshape(Bx, Tx, H, HD).transpose(0, 2, 1, 3)
        k = jnp.einsum('btd,od->bto', x, Wk).reshape(Bx, Tx, G, HD).transpose(0, 2, 1, 3)
        v = jnp.einsum('btd,od->bto', x, Wv).reshape(Bx, Tx, G, HD).transpose(0, 2, 1, 3)
        q = _rms(q, q_norm_scale)
        k = _rms(k, k_norm_scale)
        pos = kv_lens[:, None] + jnp.arange(Tx, dtype=jnp.int32)
        q = _rope(q, pos)
        k = _rope(k, pos)
        slot = pos // BLOCK
        off = pos % BLOCK
        blk = jnp.take_along_axis(block_tables, slot, axis=1)
        k_blocks = k_blocks.at[blk, :, off, :].set(k.transpose(0, 2, 1, 3))
        v_blocks = v_blocks.at[blk, :, off, :].set(v.transpose(0, 2, 1, 3))
        k_all = k_blocks[block_tables].transpose(0, 2, 1, 3, 4).reshape(Bx, G, -1, HD)
        v_all = v_blocks[block_tables].transpose(0, 2, 1, 3, 4).reshape(Bx, G, -1, HD)
        S = k_all.shape[2]
        qg = q.reshape(Bx, G, GSZ, Tx, HD)
        scores = jnp.einsum('bghtd,bgsd->bghts', qg, k_all) * SCALE
        kpos = jnp.arange(S, dtype=jnp.int32)
        allowed = (kpos[None, None, :] <= pos[:, :, None]) & (kpos[None, None, :] > pos[:, :, None] - WINDOW)
        scores = jnp.where(allowed[:, None, None, :, :], scores, -jnp.inf)
        p = jax.nn.softmax(scores, axis=-1)
        o = jnp.einsum('bghts,bgsd->bghtd', p, v_all).reshape(Bx, H, Tx, HD)
        o = o.transpose(0, 2, 1, 3).reshape(Bx, Tx, H * HD)
        return jnp.einsum('bto,do->btd', o, Wo)

    def _L3_cond_ref(x, Wg, Wu, Wd, Ag, Bg, Au, Bu, Ad, Bd, adapter_indices):
        import jax, jax.numpy as jnp
        import numpy as np

        def _lora_linear(x, W, A, B, adapter_indices):
            base = jnp.einsum('bsd,df->bsf', x, W)
            Ai = A[adapter_indices]
            Bi = B[adapter_indices]
            lora = jnp.einsum('bsr,brf->bsf', jnp.einsum('bsd,bdr->bsr', x, Ai), Bi)
            return base + lora
        gate = _lora_linear(x, Wg, Ag, Bg, adapter_indices)
        up = _lora_linear(x, Wu, Au, Bu, adapter_indices)
        h = jax.nn.silu(gate) * up
        return _lora_linear(h, Wd, Ad, Bd, adapter_indices)
    x = x + _L0_cond_ref(x, itok_B_0_7, L0_cond_weights, fside_8xS_0)
    x = x + _L1_cond_ref(x, itok_B_0_7, L1_cond_weights)
    x = x + _L2_cond_ref(x, L2_cond_Wq, L2_cond_Wk, L2_cond_Wv, L2_cond_Wo, L2_cond_q_norm_scale, L2_cond_k_norm_scale, L2_cond_k_blocks, L2_cond_v_blocks, itok_Bx257_0_4111, itok_B_37_3939)
    x = x + _L3_cond_ref(x, L3_cond_Wg, L3_cond_Wu, L3_cond_Wd, L3_cond_Ag, L3_cond_Bg, L3_cond_Au, L3_cond_Bu, L3_cond_Ad, L3_cond_Bd, itok_B_0_7)
    return x

_drawn_inputs = setup_inputs


def setup_inputs(seed=0):
    import zlib

    import numpy as np

    out = dict(_drawn_inputs(seed))
    spreads = {'L3_cond_Bg': (0.009999999776482582, 0.6),
     'L3_cond_Bu': (0.009999999776482582, 0.6),
     'L3_cond_Bd': (0.009999999776482582, 0.6)}
    factors = {'L2_cond_q_norm_scale': 8.0,
     'L2_cond_k_norm_scale': 64.0,
     'L2_cond_k_blocks': 4.064,
     'L2_cond_Wk': 3.522}
    for name, (base, spread) in spreads.items():
        noise = np.random.default_rng([zlib.crc32(name.encode()), seed]).standard_normal(out[name].shape)
        drawn = base * np.exp(spread * noise) if base else spread * noise
        out[name] = jnp.asarray(drawn.astype(out[name].dtype))
    for name, factor in factors.items():
        out[name] = (out[name] * factor).astype(out[name].dtype)
    return out
```

```python
import numpy as np
import concourse.bass as bass
from concourse import mybir
from contextlib import ExitStack

F32 = mybir.dt.float32
BF16 = mybir.dt.bfloat16
I32 = mybir.dt.int32
ALU = mybir.AluOpType
ACT = mybir.ActivationFunctionType
AX_X = mybir.AxisListType.X

B, T, D = 64, 32, 256
NS, R = 8, 16
H, G, HD = 8, 4, 32
BLOCK, NBLK = 16, 257
NPHYS = 16 * NBLK
WINDOW = 128
KEYS = WINDOW + T
FF = 1024
P = 128
QB = P // T
NQ = B // QB
SQ = 4
NSUP = NQ // SQ
ST = SQ * P
NF = FF // P
KV = 2 * G * HD
NTOK = B * T
SCALE = 256.0 ** -0.5
EPS = 1e-6
NEG = -1e30
HALF = HD // 2
WSLOT = 3
TWN = WINDOW // BLOCK + WSLOT
NW = B * WSLOT
CBIG = 70000.0
WROW = 2 * T + 1

C_ID = 0
C_BLK = C_ID + P
C_N16 = C_BLK + QB
C_C32 = C_N16 + 1
C_EPS = C_C32 + 1
C_INV = C_EPS + 1
C_IOTA = C_INV + HALF
C_B4 = C_IOTA + NBLK
C_Q16 = C_B4 + QB
C_B32 = C_Q16 + NQ
C_ONE = C_B32 + 1
CW = C_ONE + P


def constants():
    c = np.zeros((P, CW), np.float32)
    p = np.arange(P)
    c[:, C_ID:C_ID + P] = np.eye(P)
    c[:, C_BLK:C_BLK + QB] = p[:, None] // T == np.arange(QB)
    c[:, C_N16] = p // R
    c[:, C_C32] = p % T
    c[:, C_EPS] = EPS
    c[:, C_INV:C_INV + HALF] = (1.0 / 10000.0 ** (np.arange(HALF, dtype=np.float32) / HALF)).astype(np.float32)
    c[:, C_IOTA:C_IOTA + NBLK] = np.arange(NBLK)
    c[:, C_B4:C_B4 + QB] = p[:, None] % QB == np.arange(QB)
    c[:, C_Q16:C_Q16 + NQ] = p[:, None] // QB == np.arange(NQ)
    c[:, C_B32] = T * p
    c[:, C_ONE:C_ONE + P] = 1.0
    return c


def mask_constants(bf16):
    t, r, q = np.arange(T), np.arange(KEYS), np.arange(P)
    allowed = (r[None, :] > t[:, None]) & (r[None, :] <= WINDOW + t[:, None])
    window = np.where(allowed, 0.0, NEG).astype(bf16)
    pick = np.concatenate([(q[None, :] % T == t[:, None]), np.ones((1, P))]).astype(bf16)
    return window, pick


def two_pi_parts():
    c1 = np.float32(6.28125)
    c2 = np.float32(np.round((2 * np.pi - float(c1)) * 2.0 ** 21) / 2.0 ** 21)
    c3 = np.float32(2 * np.pi - float(c1) - float(c2))
    return float(c1), float(c2), float(c3)


def wait(eng, sem, value):
    if isinstance(value, int) and value <= 0:
        return
    eng.wait_ge(sem, value)


def build(nc, x, wl, wqkv, wo, wg, wu, wd, ag, au, ad, bg, bu, bd, scales, kvpool, subj, subjq, kvlen, kvlenq, table,
          consts, window, pick, out, knew):
    ctx = ExitStack()
    with ctx:
        def sb(name, shape, dt=F32):
            return ctx.enter_context(nc.sbuf_tensor(name, shape, dt))

        def sem(name):
            return ctx.enter_context(nc.semaphore(name))

        X = sb("X", [P, NQ, D])
        XT = sb("XT", [P, 2, NTOK])
        QT = sb("QT", [P, 2, NTOK])
        C = sb("C", [P, CW])
        WL = sb("WL", [P, NQ, WROW])
        WQKV = sb("WQKV", [P, 2, 4 * P])
        WO = sb("WO", [P, 2, D])
        WG = sb("WG", [P, 2, FF])
        WU = sb("WU", [P, 2, FF])
        WD = sb("WD", [P, NF, D])
        AG = sb("AG", [P, 2, P])
        AU = sb("AU", [P, 2, P])
        AD = sb("AD", [P, NF, P])
        BG = sb("BG", [P, FF])
        BU = sb("BU", [P, FF])
        BD_ = sb("BDW", [P, D])
        SUBI = sb("SUBI", [P, B], I32)
        LMASK = sb("LMASK", [P, B])
        SUBT = sb("SUBT", [P, NQ], I32)
        WIDX = sb("WIDX", [P, NQ], I32)
        KVT = sb("KVT", [P, NQ], I32)
        KVI = sb("KVI", [B, 1], I32)
        SLOTI = sb("SLOTI", [B, 2], I32)
        SLOTF = sb("SLOTF", [B, 2])
        TABI = sb("TABI", [B, NBLK], I32)
        TABF = sb("TABF", [B, NBLK])
        TSCR = sb("TSCR", [B, 2, NBLK])
        SJ = sb("SJ", [B, TWN])
        TW = sb("TW", [B, TWN])
        TW16 = sb("TW16", [B, TWN])
        KA = sb("KA", [B, TWN, BLOCK])
        OH = sb("OH", [B, BLOCK])
        KEYT = sb("KEYT", [B, 2, KEYS])
        K1E = sb("K1E", [B, QB, T])
        LHC = sb("LHC", [B, 3, WSLOT])
        LHCE = sb("LHCE", [B, 3, WSLOT, B])
        THR = sb("THR", [B, 1])
        KVM = sb("KVM", [B, KEYS], BF16)
        KEYS_ = sb("KEYALL", [P, NQ + 4, QB + 1])
        WLHC = sb("WLHC", [P, 3, NW])
        MASK = sb("MASK", [T + 1, B, KEYS], BF16)
        PICK = sb("PICK", [T + 1, P], BF16)
        POS = sb("POS", [P, NQ])
        ANG = sb("ANG", [P, NQ, HALF])
        TR = sb("TR", [P, 2, 2, NQ, HALF])
        TRG, TRK = TR[:, 0], TR[:, 1]
        SCL = sb("SCL", [P, 2, HD])
        TCS = sb("TCS", [P, 2, NQ, 2, HD])
        TC, TS = TCS[:, 0], TCS[:, 1]
        BD0 = [sb(f"BD0_{i}", [P, QB, T]) for i in range(2)]
        BD1 = [sb(f"BD1_{i}", [P, QB, T]) for i in range(2)]
        BDT = [sb(f"BDT_{i}", [P, QB, T]) for i in range(2)]
        XA = sb("XA", [P, 4, D])
        X1 = [XA[:, i, :] for i in range(2)]
        X2S = [XA[:, 2 + i, :].rearrange("p (h t) -> p h t", h=2) for i in range(2)]
        PA = sb("PA", [P, 8, 12, HD])
        SQR, RA, RB, RS_ = ([PA[:, 2 * j + i] for i in range(2)] for j in range(4))
        SS = [sb(f"SS_{i}", [P, 3, 12]) for i in range(2)]
        QR = [sb(f"QR_{i}", [P, 8, HD]) for i in range(2)]
        KVN = [sb(f"KVN_{i}", [P, KV]) for i in range(2)]
        U1 = TR[:].rearrange("p a c n f -> p (a c n f)")[:, 0:(QB + 1) * NW].rearrange("p (j w) -> p j w", w=NW)
        U2 = sb("U2", [P, QB + 1, NW])
        CM = sb("CM", [P, 4, QB + 1])
        OIDX = [sb(f"OIDX_{i}", [P, QB], I32) for i in range(SQ)]
        NIDX = [sb(f"NIDX_{i}", [P, QB + 1], I32) for i in range(SQ)]
        KV0 = [sb(f"KV0_{i}", [P, QB, KV]) for i in range(SQ)]
        KV1 = [sb(f"KV1_{i}", [P, KV]) for i in range(SQ)]
        QBD = [sb(f"QBD_{i}", [P, QB, 2, P]) for i in range(2)]
        KT = sb("KT", [P, QB, KEYS])
        MX = sb("MX", [P, QB, 2])
        NB = sb("NB", [P, QB, 2])
        RSUM = sb("RSM", [P, QB, 2])
        RINV = sb("RINV", [P, QB, 2])
        paf = PA[:].rearrange("p i h d -> p (i h d)")
        pw = QB * 2 * KEYS
        PE_ = paf[:, 0:pw].rearrange("p (b g r) -> p b g r", b=QB, g=2)
        PR0 = paf[:, pw:pw + 8 * P].rearrange("p (b g r) -> p b g r", b=QB, g=2)
        PR1 = paf[:, pw + 8 * P:2 * pw].rearrange("p (g b r) -> p g b r", g=2, b=QB)
        PT0 = XA[:].rearrange("p i d -> p (i d)").rearrange("p (b g q) -> p b g q", b=QB, g=2)
        V1M = [WL[:].rearrange("p n c -> p (n c)")[:, ST * i:ST * i + ST].rearrange("p (b c) -> p b c", b=QB) for i in range(2)]
        GATE = sb("GATE", [P, 1])
        PT1 = sb("PT1", [P, 2, P])
        OT = sb("OT", [P, 2, QB, T])
        ZG, ZU, ZD, TH, GA, *HB = (X[:].rearrange("p n d -> p (n d)")[:, ST * i:ST * i + ST] for i in range(7))
        X4, OUTB = (TCS[:, i].rearrange("p n a d -> p (n a d)").rearrange("p (n d) -> p n d", n=n) for i, n in ((0, 2), (1, SQ)))

        PS = ctx.enter_context(nc.psum_tensor("PS", [P, 8, 512], F32))
        ring = PS[:, 5:8, :]

        def cc(at, n=1, rows=P):
            return C[0:rows, at:at + n]

        s_const, s_idx, s_x, s_wa, s_wb, s_bc = (sem(n) for n in ("s_const", "s_idx", "s_x", "s_wa", "s_wb", "s_bc"))
        s_set = sem("s_set")
        s_widx = sem("s_widx")
        s_wl = sem("s_wl")
        s_kvm = sem("s_kvm")
        s_mask = sem("s_mask")
        s_keyt = sem("s_keyt")
        s_lhce = sem("s_lhce")
        s_keyps = sem("s_keyps")
        s_keysb = sem("s_keysb")
        s_arg = sem("s_arg")
        s_trg = sem("s_trg")
        s_bd = sem("s_bd")
        s_l0 = sem("s_l0")
        s_x1 = sem("s_x1")
        s_l1 = sem("s_l1")
        s_x2 = sem("s_x2")
        s_qkv = sem("s_qkv")
        s_sq = sem("s_sq")
        s_ss = sem("s_ss")
        s_rt = sem("s_rt")
        s_ab = sem("s_ab")
        s_ri = sem("s_ri")
        s_rs = sem("s_rs")
        s_rot = sem("s_rot")
        s_vc = sem("s_vc")
        s_kst = [sem("s_kst0"), sem("s_kst1")]
        s_qt = sem("s_qt")
        s_qts = sem("s_qts")
        s_dve = sem("s_dve")
        s_zero = sem("s_zero")
        s_oidx, s_nidx = sem("s_oidx"), sem("s_nidx")
        s_old = [sem(f"s_old{i}") for i in range(SQ)]
        s_new = [sem(f"s_new{i}") for i in range(SQ)]
        s_gate = sem("s_gate")
        s_vm = sem("s_vm")
        s_qbd = sem("s_qbd")
        s_ktp, s_kt0, s_kt1 = sem("s_ktp"), sem("s_kt0"), sem("s_kt1")
        s_sc, s_mx, s_nb, s_ex, s_rinv, s_pr = (sem(n) for n in ("s_sc", "s_mx", "s_nb", "s_ex", "s_rinv", "s_pr"))
        s_ptp, s_ptd, s_pta = sem("s_ptp"), sem("s_ptd"), sem("s_pta")
        s_av, s_otd, s_ota = sem("s_av"), sem("s_otd"), sem("s_ota")
        s_wo, s_x3 = sem("s_wo"), sem("s_x3")
        s_la, s_z = sem("s_la"), sem("s_z")
        s_g, s_u, s_th, s_ga, s_h, s_dn = (sem(n) for n in ("s_g", "s_u", "s_th", "s_ga", "s_h", "s_dn"))
        s_m1, s_m2, s_m3, s_m4 = (sem(n) for n in ("s_m1", "s_m2", "s_m3", "s_m4"))
        s_zd, s_y, s_x4, s_yt, s_ob, s_out = (sem(n) for n in ("s_zd", "s_y", "s_x4", "s_yt", "s_ob", "s_out"))

        block = ctx.enter_context(nc.Block())

        def phase_a(eng, step, first, last, lo=4, hi=NQ):
            for k in range(first, lo):
                step(k)
            with eng.Fori(lo // 2, hi // 2) as it:
                for u in range(2):
                    step(it * 2 + u, u)
            for k in range(hi, last + 1):
                step(k)

        def has(n):
            return not isinstance(n, int) or 0 <= n < NQ

        def phase_b(eng, step):
            for u in range(SQ):
                step(0, u, True, False)
            with eng.Fori(1, NSUP) as it:
                for u in range(SQ):
                    step(it, u, True, True)
            for u in range(SQ):
                step(NSUP, u, False, True)

        @block.sync
        def _(sp):
            for dst, src in ((TABI[:], table), (KVI[:], kvlen.rearrange("(b o) -> b o", o=1)), (C[:], consts)):
                sp.dma_start(dst, src).then_inc(s_idx, 16)
            for j in range(QB):
                rows = slice(T * j, T * j + T)
                sp.dma_start(SUBT[rows, :], subjq[j:j + 1, :].broadcast_to([T, NQ])).then_inc(s_bc, 16)
                sp.dma_start(KVT[rows, :], kvlenq[j:j + 1, :].broadcast_to([T, NQ])).then_inc(s_bc, 16)
            sp.dma_start(SUBI[:], subj.rearrange("(o b) -> o b", o=1).broadcast_to([P, B])).then_inc(s_bc, 16)
            sp.dma_start(SCL[:].rearrange("p a d -> p (a d)"), scales.rearrange("(o n) -> o n", o=1).broadcast_to([P, 2 * HD])).then_inc(s_bc, 16)
            sp.dma_start(X[:], x.rearrange("(n p) d -> p n d", p=P)).then_inc(s_x, 16)
            sp.dma_start(WQKV[:], wqkv).then_inc(s_wa, 16)
            sp.dma_start(WO[:], wo).then_inc(s_wa, 16)
            sp.dma_start(PICK[:], pick).then_inc(s_mask, 16)
            sp.dma_start(MASK[0:T, :, :], window.rearrange("t (o r) -> t o r", o=1).broadcast_to([T, B, KEYS])).then_inc(s_mask, 16)
            sp.wait_ge(s_kvm, 1)
            sp.dma_start(MASK[T:T + 1, :, :], KVM[:, :]).then_inc(s_mask, 16)
            for dst, src in ((WG, wg), (WU, wu), (WD, wd), (AG, ag), (AU, au), (AD, ad), (BG, bg), (BU, bu), (BD_, bd)):
                sp.dma_start(dst[:], src).then_inc(s_wb, 16)

            def store_new(n, u):
                wait(sp, s_rot, n + 1)
                wait(sp, s_vc, n + 1)
                sp.dma_start(knew[bass.ds(n * P, P), :], KVN[u][:]).then_inc(s_kst[u], 16)

            with sp.Fori(0, NQ // 2) as it:
                for u in range(2):
                    store_new(it * 2 + u, u)
            for s in range(NSUP):
                sp.wait_ge(s_ob, 2 * s + 2)
                sp.dma_start(out[s * ST:(s + 1) * ST, :].rearrange("(n p) d -> p n d", p=P), OUTB[:]).then_inc(s_out, 16)
            sp.wait_ge(s_out, 16 * NSUP)

        @block.gpsimd
        def _(pool):
            nc.gpsimd.memset(KEYS_[:], 0.0).then_inc(s_zero, 1)
            pool.wait_ge(s_widx, 1)
            for n in range(NQ):
                nc.gpsimd.indirect_dma_start(WL[:, n, :], None, wl, bass.IndirectOffsetOnAxis(WIDX[:, n:n + 1], 0)).then_inc(s_wl, 16)

            def rotate(k, u=None):
                n = k - 2
                i = (k if u is None else u) % 2
                if not has(n):
                    return
                wait(pool, s_ab, n + 1)
                wait(pool, s_rot, n - 1)
                nc.gpsimd.tensor_tensor(RS_[i][:], RA[i][:], RB[i][:], ALU.add).then_inc(s_rs, 1)
                wait(pool, s_rs, n + 1)
                wait(pool, s_ri, n + 1)
                wait(pool, s_qt, n - 1)
                if not isinstance(n, int):
                    pool.wait_ge(s_kst[i], (n // 2) * 16 if isinstance(n, int) else half_count(n, i))
                elif n >= 2:
                    pool.wait_ge(s_kst[i], 16 * (n // 2))
                inv = SS[i][:, 2, :]
                nc.gpsimd.tensor_tensor(QR[i][:], RS_[i][:, 0:8, :], inv[:, 0:8].unsqueeze(2).broadcast_to([P, 8, HD]), ALU.mult)
                nc.gpsimd.tensor_tensor(KVN[i][:, 0:P].rearrange("p (h d) -> p h d", h=G), RS_[i][:, 8:12, :],
                                        inv[:, 8:12].unsqueeze(2).broadcast_to([P, G, HD]), ALU.mult).then_inc(s_rot, 1)

            def half_count(n, i):
                return (n - i) * 8

            phase_a(pool, rotate, 2, NQ + 1)

            def gate(passed):
                wait(pool, s_gate, passed)
                nc.gpsimd.tensor_tensor(GATE[:], cc(C_EPS), cc(C_EPS), ALU.add).then_inc(s_gate, 1)

            def old(it, u):
                k = it * SQ + u
                wait(pool, s_oidx, k + 1)
                wait(pool, s_av, k - SQ + 1)
                gate(2 * k)
                for j in range(QB):
                    nc.gpsimd.indirect_dma_start(KV0[u][:, j, :], None, kvpool,
                                                 bass.IndirectOffsetOnAxis(OIDX[u][:, j:j + 1], 0)).then_inc(s_old[u], 16)

            def new(it, u):
                k = it * SQ + u
                wait(pool, s_nidx, k + 1)
                wait(pool, s_old[u], (it + 1) * 16 * QB)
                gate(2 * k + 1)
                for j in range(QB):
                    nc.gpsimd.indirect_dma_start(KV0[u][:, j, :], None, knew, bass.IndirectOffsetOnAxis(NIDX[u][:, j:j + 1], 0),
                                                 bounds_check=NTOK - 1, oob_is_err=False).then_inc(s_new[u], 16)
                nc.gpsimd.indirect_dma_start(KV1[u][:], None, knew, bass.IndirectOffsetOnAxis(NIDX[u][:, QB:QB + 1], 0)).then_inc(s_new[u], 16)

            def spread_q(it, u):
                k = it * SQ + u
                wait(pool, s_sc, QB * (k - 1))
                wait(pool, s_qts, k + 1)
                for b in range(QB):
                    src = QT[:, :, bass.ds(k * P + b * T, T)].unsqueeze(1).broadcast_to([P, G, 2, T])
                    nc.gpsimd.tensor_tensor(QBD[u % 2][:, b, :, :].rearrange("p c (g h t) -> p (c g) h t", g=2, h=2), src,
                                            cc(C_BLK, G).unsqueeze(2).unsqueeze(3).broadcast_to([P, G, 2, T]), ALU.mult).then_inc(s_qbd, 1)

            def part_v(it, u):
                k = it * SQ + u
                wait(pool, s_new[u], (it + 1) * 16 * (QB + 1))
                wait(pool, s_av, k - 1)
                nc.gpsimd.tensor_tensor(V1M[u % 2], KV1[u][:, P:KV].unsqueeze(1).broadcast_to([P, QB, P]),
                                        cc(C_BLK, QB).unsqueeze(2).broadcast_to([P, QB, P]), ALU.mult).then_inc(s_vm, 1)

            old(0, 0)
            for i in range(2):
                pool.wait_ge(s_kst[i], 16 * NQ // 2)
            spread_q(0, 0)
            new(0, 0)
            for u in range(1, SQ):
                old(0, u)
                spread_q(0, u)
                part_v(0, u - 1)
                new(0, u)
            with pool.Fori(1, NSUP) as it:
                for u in range(SQ):
                    old(it, u)
                    spread_q(it, u)
                    part_v(it if u else it - 1, (u - 1) % SQ)
                    new(it, u)
            part_v(NSUP - 1, SQ - 1)

        @block.scalar
        def _(act):
            act.wait_ge(s_arg, 1)
            nc.scalar.activation(TRG[:], TRK[:], ACT.Sin).then_inc(s_trg, 1)

            def step_a(k, u=None):
                par = (k if u is None else u) % 2
                n, i = k - 1, (par + 1) % 2
                if has(n):
                    wait(act, s_l1, n + 1)
                    wait(act, s_qkv, n - 1)
                    src = PS[:, 2 + i, 0:D].rearrange("p (h t) -> p h t", h=2)
                    nc.scalar.activation(X2S[i][:], src, ACT.Copy)
                    nc.scalar.activation(XT[:, :, bass.ds(n * P, P)], src, ACT.Copy).then_inc(s_x2, 1)
                n, i = k - 2, par
                if has(n):
                    wait(act, s_qkv, n + 1)
                    wait(act, s_ss, n - 1)
                    nc.scalar.activation(SQR[i][:], PS[:, 4 + i, 0:12 * HD].rearrange("p (h d) -> p h d", h=12), ACT.Square).then_inc(s_sq, 1)
                    if not isinstance(n, int):
                        act.wait_ge(s_kst[i], (n - i) * 8)
                    elif n >= 2:
                        act.wait_ge(s_kst[i], 16 * (n // 2))
                    nc.scalar.activation(KVN[i][:, P:KV], PS[:, 4 + i, 12 * HD:16 * HD], ACT.Copy).then_inc(s_vc, 1)
                    wait(act, s_ss, n + 1)
                    nc.scalar.activation(SS[i][:, 1, :], SS[i][:, 0, :], ACT.Sqrt, bias=cc(C_EPS), scale=1.0 / HD).then_inc(s_rt, 1)
                n = k - 3
                if has(n):
                    wait(act, s_qt, n + 1)
                    nc.scalar.activation(QT[:, :, bass.ds(n * P, P)], PS[:, 6, 0:D].rearrange("p (h t) -> p h t", h=2), ACT.Copy).then_inc(s_qts, 1)

            phase_a(act, step_a, 1, NQ + 2)

            def tanh(F):
                wait(act, s_g, F + 1)
                wait(act, s_ga, F)
                nc.scalar.activation(TH[:], PS[:, 0, :], ACT.Tanh, scale=0.5).then_inc(s_th, 1)

            def step_b(it, u, attn, mlp):
                k = it * SQ + u
                F = (it - 1) * NF + 2 * u
                if attn:
                    wait(act, s_ktp, 2 * k + 2)
                    wait(act, s_sc, QB * k)
                    nc.scalar.activation(KT[:, :, P:KEYS], ring[:, 1, 0:P].rearrange("p (b r) -> p b r", b=QB), ACT.Copy).then_inc(s_kt1, 1)
                if mlp:
                    tanh(F)
                if attn:
                    for b in range(QB):
                        wait(act, s_nb, QB * k + b + 1)
                        if b == 0:
                            wait(act, s_pr, k)
                        for gp in range(2):
                            nc.scalar.activation(PE_[:, b, gp, :], ring[:, (2 + b) % 3, KEYS * gp:KEYS * gp + KEYS], ACT.Exp,
                                                 bias=NB[:, b, gp:gp + 1], scale=SCALE,
                                                 accum_out=RSUM[:, b, gp:gp + 1]).then_inc(s_ex, 1)
                if mlp:
                    tanh(F + 1)
                if attn:
                    wait(act, s_ptp, 3 * k + 2)
                    wait(act, s_av, k)
                    nc.scalar.activation(PT0[:, 2:4, :, :].rearrange("p b g q -> p (b g q)"), ring[:, 1, :], ACT.Copy).then_inc(s_pta, 1)
                if mlp and u == SQ - 1:
                    for j in range(2):
                        wait(act, s_yt, 2 * (it - 1) + j + 1)
                        wait(act, s_out, 16 * (it - 1))
                        nc.scalar.activation(OUTB[:, 2 * j:2 * j + 2, :].rearrange("p n d -> p (n d)"), PS[:, j, :], ACT.Copy).then_inc(s_ob, 1)
                if attn:
                    wait(act, s_av, k + 1)
                    wait(act, s_wo, k)
                    for g in (2, 3):
                        diag(nc.scalar.copy, g).then_inc(s_ota, 1)

            def diag(copy, g):
                src = ring[T * g:T * g + T, 0:2, :].rearrange("p i (b q) -> p (i b) q", b=2)[:, :, 64 * g:64 * g + 64]
                return copy(OT[T * g:T * g + T, :, :, :].rearrange("p h b t -> p b h t"), src.rearrange("p b (h t) -> p b h t", h=2))

            phase_b(act, step_b)

        @block.vector
        def _(dve):
            done = [0]

            def link(ins):
                done[0] += 1
                ins.then_inc(s_set, 1)
                dve.wait_ge(s_set, done[0])

            v = nc.vector
            dve.wait_ge(s_idx, 48)
            dve.wait_ge(s_bc, 160)
            link(v.tensor_scalar(POS[:], SUBT[:], float(T), cc(C_C32), ALU.mult, ALU.add))
            v.tensor_copy(WIDX[:], POS[:]).then_inc(s_widx, 1)
            v.tensor_scalar(LMASK[:], SUBI[:], cc(C_N16), None, ALU.is_equal)
            v.tensor_scalar(SLOTI[:, 0:1], KVI[:], 4, None, ALU.logical_shift_right)
            v.tensor_scalar(SLOTI[:, 1:2], KVI[:], 15, None, ALU.bitwise_and)
            v.tensor_copy(TABF[:], TABI[:])
            link(v.tensor_scalar(THR[:], KVI[:], -1.0, float(WINDOW), ALU.mult, ALU.add))
            v.tensor_scalar(KVM[:], cc(C_IOTA, KEYS, B), THR[:, 0:1], NEG, ALU.is_lt, ALU.mult).then_inc(s_kvm, 1)
            link(v.tensor_copy(SLOTF[:], SLOTI[:]))
            v.tensor_scalar(OH[:], cc(C_IOTA, BLOCK, B), SLOTF[:, 1:2], None, ALU.is_equal)
            link(v.tensor_scalar(SJ[:], cc(C_IOTA, TWN, B), SLOTF[:, 0:1], float(-(WINDOW // BLOCK)), ALU.add, ALU.add))
            for j in range(TWN):
                link(v.scalar_tensor_tensor(TSCR[:, j % 2, :], cc(C_IOTA, NBLK, B), SJ[:, j:j + 1], TABF[:], ALU.is_equal, ALU.mult,
                                            accum_out=TW[:, j:j + 1]))
            link(v.tensor_scalar(TW16[:], TW[:], float(BLOCK), None, ALU.mult))
            link(v.tensor_tensor(KA[:], TW16[:].unsqueeze(2).broadcast_to([B, TWN, BLOCK]),
                                 cc(C_IOTA, BLOCK, B).unsqueeze(1).broadcast_to([B, TWN, BLOCK]), ALU.add))
            kaf = KA[:].rearrange("b j o -> b (j o)")
            link(v.tensor_scalar(KEYT[:, 0, :], kaf[:, 0:KEYS], OH[:, 0:1], None, ALU.mult))
            for m in range(1, BLOCK):
                link(v.scalar_tensor_tensor(KEYT[:, m % 2, :], kaf[:, m:m + KEYS], OH[:, m:m + 1], KEYT[:, (m - 1) % 2, :], ALU.mult, ALU.add))
            keyt = KEYT[:, (BLOCK - 1) % 2, :]
            v.tensor_tensor(K1E[:], keyt[:, P:KEYS].unsqueeze(1).broadcast_to([B, QB, T]),
                            cc(C_B4, QB, B).unsqueeze(2).broadcast_to([B, QB, T]), ALU.mult).then_inc(s_keyt, 1)
            rem = SLOTF[:, 1:2]
            last = TW16[:, TWN - WSLOT:TWN]
            v.tensor_copy(LHC[:, 0, 1:3], last[:, 1:3])
            v.tensor_scalar(LHC[:, 0, 0:1], last[:, 0:1], rem, None, ALU.add)
            v.tensor_scalar(LHC[:, 1, 0:2], last[:, 0:2], float(BLOCK - 1), None, ALU.add)
            v.tensor_scalar(LHC[:, 1, 2:3], last[:, 2:3], rem, -1.0, ALU.add, ALU.add)
            link(v.tensor_scalar(LHC[:, 2, :], last, -1.0, rem, ALU.mult, ALU.subtract))
            link(v.scalar_tensor_tensor(TSCR[:, 0, 0:WSLOT], cc(C_IOTA, WSLOT, B), float(BLOCK), LHC[:, 2, :], ALU.mult, ALU.add))
            link(v.tensor_scalar(LHC[:, 2, :], TSCR[:, 0, 0:WSLOT], cc(C_B32, 1, B), CBIG, ALU.add, ALU.add))
            v.tensor_tensor(LHCE[:].rearrange("b x i c -> b (x i) c"),
                            LHC[:].rearrange("b x i -> b (x i)").unsqueeze(2).broadcast_to([B, 3 * WSLOT, B]),
                            cc(C_ID, B, B).unsqueeze(1).broadcast_to([B, 3 * WSLOT, B]), ALU.mult).then_inc(s_lhce, 1)
            dve.wait_ge(s_keyps, 4)
            dve.wait_ge(s_zero, 1)
            v.tensor_copy(KEYS_[:, 0:NQ, 0:QB], PS[:, 7, 0:B].rearrange("p (n j) -> p n j", j=QB))
            v.tensor_copy(KEYS_[:, 0:NQ, QB], PS[:, 7, B:B + NQ])
            v.tensor_copy(WLHC[:, 0:2, :].rearrange("p x w -> p (x w)"), PS[:, 6, 0:2 * NW])
            v.tensor_copy(WLHC[:, 2, :], PS[:, 5, 0:NW]).then_inc(s_keysb, 1)
            dve.wait_ge(s_keysb, 1)

            link(v.tensor_scalar(POS[:], KVT[:], cc(C_C32), None, ALU.add))
            link(v.tensor_tensor(ANG[:], POS[:].unsqueeze(2).broadcast_to([P, NQ, HALF]),
                                 cc(C_INV, HALF).unsqueeze(1).broadcast_to([P, NQ, HALF]), ALU.mult))
            magic = 1.5 * 2.0 ** 23
            c1, c2, c3 = two_pi_parts()
            v.tensor_scalar(TRG[:, 0], ANG[:], 1.0 / (2 * np.pi), 0.25, ALU.mult, ALU.add)
            link(v.tensor_scalar(TRG[:, 1], ANG[:], 1.0 / (2 * np.pi), None, ALU.mult))
            link(v.tensor_scalar(TRK[:], TRG[:], magic, None, ALU.add))
            link(v.tensor_scalar(TRG[:], TRK[:], -magic, None, ALU.add))
            for i in range(2):
                link(v.scalar_tensor_tensor(TRK[:, i], TRG[:, i], -c1, ANG[:], ALU.mult, ALU.add))
            trg, trk = (t[:].rearrange("p a n f -> p (a n f)") for t in (TRG, TRK))
            link(v.scalar_tensor_tensor(trk, trg, -c2, trk, ALU.mult, ALU.add))
            link(v.scalar_tensor_tensor(trk, trg, -c3, trk, ALU.mult, ALU.add))
            link(v.tensor_scalar(TRK[:, 0], TRK[:, 0], float(np.pi / 2), None, ALU.add))
            v.tensor_scalar(TRK[:], TRK[:], 3.1415925, -3.1415925, ALU.min, ALU.max).then_inc(s_arg, 1)
            link(v.tensor_scalar(RA[0][:, 0:2, :], SCL[:], 1.0, None, ALU.add))
            dve.wait_ge(s_trg, 1)
            one = RA[0][:, 0:2, :]
            for a in range(2):
                for h in range(2):
                    hs, other = slice(HALF * h, HALF * h + HALF), slice(HALF * (1 - h), HALF * (1 - h) + HALF)
                    v.tensor_tensor(TC[:, :, a, hs], TRG[:, 0], one[:, a, hs].unsqueeze(1).broadcast_to([P, NQ, HALF]), ALU.mult)
                    link(v.tensor_tensor(TS[:, :, a, hs], TRG[:, 1], one[:, a, other].unsqueeze(1).broadcast_to([P, NQ, HALF]), ALU.mult))
            link(v.tensor_scalar(TS[:, :, :, 0:HALF], TS[:, :, :, 0:HALF], -1.0, None, ALU.mult))

            def blocks(n, i):
                wait(dve, s_l0, n - 1)
                wait(dve, s_l1, n - 1)
                mask = cc(C_BLK, QB).unsqueeze(2).broadcast_to([P, QB, T])
                w = WL[:, bass.ds(n, 1), :].rearrange("p o c -> p (o c)")
                v.tensor_tensor(BDT[i][:], w[:, T:2 * T].unsqueeze(1).broadcast_to([P, QB, T]), mask, ALU.mult).then_inc(s_dve, 1)
                v.tensor_tensor(BD0[i][:], w[:, 0:T].unsqueeze(1).broadcast_to([P, QB, T]), mask, ALU.mult)
                wait(dve, s_dve, n + 1)
                v.tensor_tensor(BD1[i][:], BDT[i][:], cc(C_ID, P).rearrange("p (j c) -> p j c", j=QB), ALU.add).then_inc(s_bd, 1)

            def step_a(k, u=None):
                par = (k if u is None else u) % 2
                n, i = k + 1, (par + 1) % 2
                if has(n):
                    blocks(n, i)
                n, i = k, par
                if has(n):
                    wait(dve, s_l0, n + 1)
                    wait(dve, s_l1, n - 1)
                    v.scalar_tensor_tensor(X1[i][:], PS[:, i, 0:D], WL[:, bass.ds(n, 1), 2 * T:2 * T + 1].rearrange("p o c -> p (o c)"),
                                           X[:, bass.ds(n, 1), :].rearrange("p o d -> p (o d)"), ALU.add, ALU.add).then_inc(s_x1, 1)
                n, i = k - 2, par
                if has(n):
                    wait(dve, s_sq, n + 1)
                    wait(dve, s_rs, n - 1)
                    wait(dve, s_rt, n - 1)
                    v.reduce_sum(SS[i][:, 0, :], SQR[i][:], AX_X).then_inc(s_ss, 1)
                    wait(dve, s_vc, n + 1)
                    qk = PS[:, 4 + i, 0:12 * HD].rearrange("p (h d) -> p h d", h=12)
                    tc = TC[:, bass.ds(n, 1), :, :].rearrange("p o a d -> p (o a) d")
                    ts = TS[:, bass.ds(n, 1), :, :].rearrange("p o a d -> p (o a) d")
                    for a, lo, hi in ((0, 0, 8), (1, 8, 12)):
                        m = hi - lo
                        v.tensor_tensor(RA[i][:, lo:hi, :], qk[:, lo:hi, :], tc[:, a:a + 1, :].broadcast_to([P, m, HD]), ALU.mult)
                        for h in range(2):
                            hs, other = slice(HALF * h, HALF * h + HALF), slice(HALF * (1 - h), HALF * (1 - h) + HALF)
                            last = v.tensor_tensor(RB[i][:, lo:hi, hs], qk[:, lo:hi, other], ts[:, a:a + 1, hs].broadcast_to([P, m, HALF]), ALU.mult)
                    last.then_inc(s_ab, 1)
                    wait(dve, s_rt, n + 1)
                    wait(dve, s_rot, n - 1)
                    v.reciprocal(SS[i][:, 2, :], SS[i][:, 1, :]).then_inc(s_ri, 1)

            dve.wait_ge(s_wl, 16 * NQ)
            dve.wait_ge(s_x, 16)
            phase_a(dve, step_a, -1, NQ + 1, lo=4, hi=NQ - 2)

            def match(it, u):
                k = it * SQ + u
                wait(dve, s_cm, k)
                for j in range(QB + 1):
                    key = KEYS_[:, bass.ds(k, 1), j:j + 1].rearrange("p o c -> p (o c)")
                    v.scalar_tensor_tensor(U1[:, j, :], WLHC[:, 0, :], key, WLHC[:, 2, :], ALU.is_le, ALU.mult).then_inc(s_u1, 1)
                wait(dve, s_old[u], it * 16 * QB)
                v.tensor_scalar(OIDX[u][:], KEYS_[:, bass.ds(k, 1), 0:QB].rearrange("p o c -> p (o c)"), 0.0, None, ALU.add).then_inc(s_oidx, 1)
                for j in range(QB + 1):
                    key = KEYS_[:, bass.ds(k, 1), j:j + 1].rearrange("p o c -> p (o c)")
                    wait(dve, s_u1, (QB + 1) * k + j + 1)
                    last = v.scalar_tensor_tensor(U2[:, j, :], WLHC[:, 1, :], key, U1[:, j, :], ALU.is_ge, ALU.mult)
                last.then_inc(s_u2, 1)
                wait(dve, s_u2, k + 1)
                v.tensor_reduce(CM[:, 0, :], U2[:], AX_X, ALU.max).then_inc(s_c0, 1)
                wait(dve, s_c0, k + 1)
                v.tensor_scalar(CM[:, 1, :], CM[:, 0, :], 0.0, 4.0 * CBIG, ALU.is_equal, ALU.mult)
                v.tensor_tensor(CM[:, 2, :], CM[:, 0, :], KEYS_[:, bass.ds(k, 1), :].rearrange("p o c -> p (o c)"), ALU.add).then_inc(s_c1, 1)
                wait(dve, s_c1, k + 1)
                wait(dve, s_new[u], it * 16 * (QB + 1))
                v.scalar_tensor_tensor(NIDX[u][:], CM[:, 2, :], -CBIG, CM[:, 1, :], ALU.add, ALU.add).then_inc(s_nidx, 1)

            def gated(F, f, first=False):
                wait(dve, s_th, F + 1)
                wait(dve, s_h, F)
                v.scalar_tensor_tensor(GA[:], TH[:], 1.0, PS[:, 0, :], ALU.add, ALU.mult).then_inc(s_ga, 1)
                wait(dve, s_ga, F + 1)
                wait(dve, s_u, F + 1)
                if not first:
                    wait(dve, s_dn, F - 1)
                v.scalar_tensor_tensor(HB[f % 2][:], PS[:, 1, :], 0.5, GA[:], ALU.mult, ALU.mult).then_inc(s_h, 1)

            def adapters(S):
                return LMASK[:, bass.ds(S * QB * SQ, QB * SQ)].unsqueeze(2).broadcast_to([P, QB * SQ, T])

            def step_b(it, u, attn, mlp):
                k = it * SQ + u
                S = it - 1
                F = S * NF + 2 * u
                if attn:
                    wait(dve, s_ktp, 2 * k + 1)
                    wait(dve, s_sc, QB * k)
                    v.tensor_copy(KT[:, :, 0:P], ring[:, 0, :].rearrange("p (b r) -> p b r", b=QB)).then_inc(s_kt0, 1)
                if mlp:
                    if u == 0:
                        for j, z in enumerate((ZG, ZU)):
                            wait(dve, s_la, 2 * S + j + 1)
                            wait(dve, s_u, NF * S)
                            v.tensor_tensor(z[:].rearrange("p (b t) -> p b t", t=T), PS[:, j, :].rearrange("p (b t) -> p b t", t=T),
                                            adapters(S), ALU.mult).then_inc(s_z, 1)
                    gated(F, 0, u == 0)
                if attn:
                    for b in range(QB):
                        wait(dve, s_sc, QB * k + b + 1)
                        if b == 0:
                            wait(dve, s_ex, 2 * QB * k)
                        v.reduce_max(MX[:, b, :], ring[:, (2 + b) % 3, 0:2 * KEYS].rearrange("p (g r) -> p g r", g=2), AX_X).then_inc(s_mx, 1)
                        wait(dve, s_mx, QB * k + b + 1)
                        v.tensor_scalar(NB[:, b, :], MX[:, b, :], -SCALE, None, ALU.mult).then_inc(s_nb, 1)
                    wait(dve, s_ex, 2 * QB * (k + 1))
                    v.reciprocal(RINV[:].rearrange("p b g -> p (b g)"), RSUM[:].rearrange("p b g -> p (b g)")).then_inc(s_rinv, 1)
                    wait(dve, s_rinv, k + 1)
                    wait(dve, s_ptp, 3 * k)
                    for b in range(QB):
                        for gp in range(2):
                            v.tensor_scalar(PR0[:, b, gp, :], PE_[:, b, gp, 0:P], RINV[:, b, gp:gp + 1], None, ALU.mult)
                    v.tensor_tensor(PR1, PE_[:, :, :, P:KEYS].rearrange("p b g r -> p g b r"),
                                    RINV[:].rearrange("p b g -> p g b").unsqueeze(3).broadcast_to([P, 2, QB, T]), ALU.mult).then_inc(s_pr, 1)
                if mlp:
                    gated(F + 1, 1)
                if attn:
                    wait(dve, s_av, k)
                    wait(dve, s_ptp, 3 * k + 1)
                    v.tensor_copy(PT0[:, 0:2, :, :].rearrange("p b g q -> p (b g q)"), ring[:, 0, :])
                    wait(dve, s_ptp, 3 * k + 3)
                    v.tensor_copy(PT1[:].rearrange("p g q -> p (g q)"), ring[:, 2, 0:2 * P]).then_inc(s_ptd, 1)
                if mlp and u == SQ - 1:
                    wait(dve, s_dn, NF * S + NF)
                    wait(dve, s_y, S)
                    v.tensor_tensor(ZD[:].rearrange("p (b t) -> p b t", t=T), PS[:, 4, :].rearrange("p (b t) -> p b t", t=T),
                                    adapters(S), ALU.mult).then_inc(s_zd, 1)
                    wait(dve, s_y, S + 1)
                    wait(dve, s_yt, 2 * S)
                    v.tensor_tensor(X4[:], PS[:, 2:4, :], XT[:, :, bass.ds(S * ST, ST)], ALU.add).then_inc(s_x4, 1)
                if attn:
                    wait(dve, s_av, k + 1)
                    wait(dve, s_wo, k)
                    for g in (0, 1):
                        src = ring[T * g:T * g + T, 0:2, :].rearrange("p i (b q) -> p (i b) q", b=2)[:, :, 64 * g:64 * g + 64]
                        last = v.tensor_copy(OT[T * g:T * g + T, :, :, :].rearrange("p h b t -> p b h t"), src.rearrange("p b (h t) -> p b h t", h=2))
                    last.then_inc(s_otd, 1)
                    wait(dve, s_wo, k + 1)
                    xq = XT[:, :, bass.ds(k * P, P)]
                    v.tensor_tensor(xq, ring[:, 2, 0:2 * P].rearrange("p (h t) -> p h t", h=2), xq, ALU.add).then_inc(s_x3, 1)
                    match(it + (u + 2) // SQ, (u + 2) % SQ)

            s_cm, s_u1, s_u2, s_c0, s_c1 = s_nidx, s_m1, s_m2, s_m3, s_m4
            match(0, 0)
            match(0, 1)
            phase_b(dve, step_b)

        @block.tensor
        def _(pe):
            mm = nc.tensor.matmul
            ident = cc(C_ID, P)

            def tr(o, i):
                return nc.tensor.transpose(o, i, ident[0:i.shape[0], 0:i.shape[0]])

            pe.wait_ge(s_idx, 48)
            keyt = KEYT[:, (BLOCK - 1) % 2, :]
            pe.wait_ge(s_keyt, 1)
            tr(PS[:, 7, 0:B], keyt[:, 0:P]).then_inc(s_keyps, 1)
            mm(PS[:, 7, B:B + NQ], K1E[:].rearrange("b j t -> b (j t)"), cc(C_Q16, NQ, B), start=True, stop=True).then_inc(s_keyps, 1)
            pe.wait_ge(s_lhce, 1)
            e = LHCE[:].rearrange("b x i c -> b (x i c)")
            mm(PS[:, 6, 0:2 * NW], cc(C_ONE, P, B), e[:, 0:2 * NW], start=True, stop=True).then_inc(s_keyps, 1)
            mm(PS[:, 5, 0:NW], cc(C_ONE, P, B), e[:, 2 * NW:3 * NW], start=True, stop=True).then_inc(s_keyps, 1)

            pe.wait_ge(s_x, 16)
            pe.wait_ge(s_wa, 32)
            pe.wait_ge(s_keysb, 1)

            def step_a(k, u=None):
                par = (k if u is None else u) % 2
                n, i = k, par
                if has(n):
                    wait(pe, s_bd, n + 1)
                    wait(pe, s_x1, n - 1)
                    mm(PS[:, i, 0:D], BD0[i][:].rearrange("p j c -> p (j c)"), X[:, bass.ds(n, 1), :], start=True, stop=True).then_inc(s_l0, 1)
                n, i = k - 1, (par + 1) % 2
                if has(n):
                    wait(pe, s_x1, n + 1)
                    wait(pe, s_x2, n - 1)
                    for h in range(2):
                        last = mm(PS[:, 2 + i, P * h:P * h + P], X1[i][:, P * h:P * h + P], BD1[i][:].rearrange("p j c -> p (j c)"), start=True, stop=True)
                    last.then_inc(s_l1, 1)
                n, i = k - 2, par
                if has(n):
                    wait(pe, s_x2, n + 1)
                    wait(pe, s_ab, n - 1)
                    wait(pe, s_vc, n - 1)
                    for h in range(2):
                        last = mm(PS[:, 4 + i, :], X2S[i][:, h, :], WQKV[:, h, :], start=h == 0, stop=h == 1)
                    last.then_inc(s_qkv, 1)
                n, i = k - 3, (par + 1) % 2
                if has(n):
                    wait(pe, s_rot, n + 1)
                    wait(pe, s_qts, n)
                    for h in range(2):
                        last = tr(PS[:, 6, P * h:P * h + P], QR[i][:, G * h:G * h + G, :].rearrange("p h d -> p (h d)"))
                    last.then_inc(s_qt, 1)

            phase_a(pe, step_a, 0, NQ + 2)
            pe.wait_ge(s_qts, NQ)
            pe.wait_ge(s_ab, NQ)
            pe.wait_ge(s_vc, NQ)
            pe.wait_ge(s_x2, NQ)
            pe.wait_ge(s_mask, 48)
            pe.wait_ge(s_wb, 144)

            def up(S, f):
                F = S * NF + f
                fs = slice(P * f, P * f + P)
                for bank, w, b, z, s, free in ((0, WG, BG, ZG, s_g, s_ga), (1, WU, BU, ZU, s_u, s_h)):
                    wait(pe, free, F)
                    if f == 0:
                        wait(pe, s_z, 2 * S + 2)
                    for h in range(2):
                        mm(PS[:, bank, :], w[:, h, fs], XT[:, h, bass.ds(S * ST, ST)], start=h == 0, stop=False)
                    mm(PS[:, bank, :], b[:, fs], z[:], start=False, stop=True).then_inc(s, 1)

            def down(S, f):
                F = S * NF + f
                wait(pe, s_h, F + 1)
                if f == 0:
                    wait(pe, s_x4, S)
                    wait(pe, s_zd, S)
                for h in range(2):
                    mm(PS[:, 2 + h, :], WD[:, f, P * h:P * h + P], HB[f % 2][:], start=f == 0, stop=False)
                mm(PS[:, 4, :], AD[:, f, :], HB[f % 2][:], start=f == 0, stop=f == NF - 1).then_inc(s_dn, 1)

            def step_b(it, u, attn, mlp):
                k = it * SQ + u
                S = it - 1
                if attn:
                    wait(pe, s_new[u], (it + 1) * 16 * (QB + 1))
                    wait(pe, s_otd, k)
                    wait(pe, s_ota, 2 * k)
                    for b in range(QB):
                        last = tr(ring[:, 0, P * b:P * b + P], KV0[u][:, b, 0:P])
                    last.then_inc(s_ktp, 1)
                    tr(ring[:, 1, 0:P], KV1[u][:, 0:P]).then_inc(s_ktp, 1)
                if mlp:
                    if u == 0:
                        wait(pe, s_x3, SQ * (S + 1))
                        wait(pe, s_ob, 2 * S)
                        for bank, a in ((0, AG), (1, AU)):
                            for h in range(2):
                                last = mm(PS[:, bank, :], a[:, h, :], XT[:, h, bass.ds(S * ST, ST)], start=h == 0, stop=h == 1)
                            last.then_inc(s_la, 1)
                    up(S, 2 * u)
                    if u > 0:
                        down(S, 2 * u - 1)
                if attn:
                    wait(pe, s_kt0, k + 1)
                    wait(pe, s_kt1, k + 1)
                    wait(pe, s_qbd, G * (k + 1))
                    for b in range(QB):
                        if b == 0:
                            wait(pe, s_x3, k)
                        if b == 3:
                            wait(pe, s_ex, 2 * QB * k + 2)
                        for gp in range(2):
                            o = ring[:, (2 + b) % 3, KEYS * gp:KEYS * gp + KEYS]
                            mm(o, QBD[u % 2][:, b, gp, :], KT[:, b, :], start=True, stop=False)
                            last = mm(o, PICK[:], MASK[:, bass.ds(k * QB + b, 1), :], start=False, stop=True)
                        last.then_inc(s_sc, 1)
                if mlp:
                    up(S, 2 * u + 1)
                    down(S, 2 * u)
                if attn:
                    wait(pe, s_pr, k + 1)
                    wait(pe, s_ex, 2 * QB * (k + 1))
                    for b in range(QB):
                        for gp in range(2):
                            j = 2 * b + gp
                            last = tr(ring[:, j // 4, P * (j % 4):P * (j % 4) + P], PR0[:, b, gp, :])
                        if b % 2:
                            last.then_inc(s_ptp, 1)
                    for gp in range(2):
                        last = tr(ring[:, 2, P * gp:P * gp + P], PR1[:, gp, :, :].rearrange("p b r -> p (b r)"))
                    last.then_inc(s_ptp, 1)
                if mlp and u == SQ - 1:
                    down(S, NF - 1)
                    wait(pe, s_zd, S + 1)
                    for h in range(2):
                        last = mm(PS[:, 2 + h, :], BD_[:, P * h:P * h + P], ZD[:], start=False, stop=True)
                    last.then_inc(s_y, 1)
                    wait(pe, s_x4, S + 1)
                    for j in range(2):
                        for n in range(2):
                            for h in range(2):
                                last = tr(PS[:, j, D * n + P * h:D * n + P * h + P], X4[:, h, P * (2 * j + n):P * (2 * j + n) + P])
                        last.then_inc(s_yt, 1)
                if attn:
                    wait(pe, s_ptd, k + 1)
                    wait(pe, s_pta, k + 1)
                    wait(pe, s_vm, k + 1)
                    for b in range(QB):
                        o = ring[:, b // 2, D * (b % 2):D * (b % 2) + D]
                        mm(o, KV0[u][:, b, P:KV], PT0[:, b, :, :].rearrange("p g q -> p (g q)"), start=True, stop=False)
                        last = mm(o, V1M[u % 2][:, b, :], PT1[:].rearrange("p g q -> p (g q)"), start=False, stop=True)
                    last.then_inc(s_av, 1)
                    wait(pe, s_otd, k + 1)
                    wait(pe, s_ota, 2 * k + 2)
                    for h in range(2):
                        for hl in range(2):
                            last = mm(ring[:, 2, P * h:P * h + P], WO[:, hl, P * h:P * h + P], OT[:, hl, :, :].rearrange("p b t -> p (b t)"),
                                      start=hl == 0, stop=hl == 1)
                    last.then_inc(s_wo, 1)

            phase_b(pe, step_b)


def kernel(x, itok_B_0_7, fside_8xS_0, itok_Bx257_0_4111, itok_B_37_3939, L0_cond_weights, L1_cond_weights,
           L2_cond_Wq, L2_cond_Wk, L2_cond_Wv, L2_cond_Wo, L2_cond_q_norm_scale, L2_cond_k_norm_scale,
           L2_cond_k_blocks, L2_cond_v_blocks, L3_cond_Wg, L3_cond_Wu, L3_cond_Wd, L3_cond_Ag, L3_cond_Bg,
           L3_cond_Au, L3_cond_Bu, L3_cond_Ad, L3_cond_Bd):
    import ml_dtypes
    import concourse.bacc as bacc
    from concourse.bass_utils import run_bass_kernel_spmd

    def lay(a, *shape):
        return np.ascontiguousarray(np.asarray(a).reshape(shape))

    def flip(a, *order):
        return np.ascontiguousarray(np.transpose(np.asarray(a), order))

    wq = flip(lay(L2_cond_Wq, G, 2, HD, D), 3, 1, 0, 2).reshape(D, P * 2)
    wk, wv = flip(L2_cond_Wk, 1, 0), flip(L2_cond_Wv, 1, 0)
    wqkv = flip(np.concatenate([wq, wk, wv], 1).reshape(2, P, 4 * P), 1, 0, 2)
    wo = flip(lay(L2_cond_Wo, D, G, 2, HD), 1, 3, 2, 0).reshape(P, 2, D)

    def rows(w, n):
        return flip(lay(w, n, P, -1), 1, 0, 2)

    def low(a, n):
        return rows(flip(a, 1, 0, 2).reshape(n * P, P), n)

    kvpool = np.concatenate([flip(L2_cond_k_blocks, 0, 2, 1, 3).reshape(NPHYS * BLOCK, P),
                             flip(L2_cond_v_blocks, 0, 2, 1, 3).reshape(NPHYS * BLOCK, P)], 1)
    wl = np.concatenate([lay(L0_cond_weights, NS * T, T), lay(L1_cond_weights, NS * T, T), lay(fside_8xS_0, NS * T, 1)], 1)
    window, pick = mask_constants(ml_dtypes.bfloat16)
    arrays = {
        "x": lay(x, NTOK, D), "wl": wl, "wqkv": wqkv, "wo": wo,
        "wg": rows(L3_cond_Wg, 2), "wu": rows(L3_cond_Wu, 2), "wd": rows(L3_cond_Wd, NF),
        "ag": low(L3_cond_Ag, 2), "au": low(L3_cond_Au, 2), "ad": low(L3_cond_Ad, NF),
        "bg": lay(L3_cond_Bg, P, FF), "bu": lay(L3_cond_Bu, P, FF), "bd": lay(L3_cond_Bd, P, D),
        "scales": np.concatenate([np.asarray(L2_cond_q_norm_scale), np.asarray(L2_cond_k_norm_scale)]),
        "kvpool": kvpool, "subj": lay(itok_B_0_7, B), "subjq": flip(lay(itok_B_0_7, NQ, QB), 1, 0),
        "kvlen": lay(itok_B_37_3939, B), "kvlenq": flip(lay(itok_B_37_3939, NQ, QB), 1, 0),
        "table": lay(itok_Bx257_0_4111, B, NBLK),
        "consts": constants(), "window": window, "pick": pick,
    }
    nc = bacc.Bacc("TRN2", target_bir_lowering=False, num_devices=1)
    arrays = {f"in_{n}": a for n, a in arrays.items()}
    args = [nc.dram_tensor(n, a.shape, mybir.dt.from_np(a.dtype), kind="ExternalInput").ap() for n, a in arrays.items()]
    out = nc.dram_tensor("out_0", (NTOK, D), F32, kind="ExternalOutput").ap()
    knew = nc.dram_tensor("k_new", (NTOK, KV), F32).ap()
    build(nc, *args, out, knew)
    r = run_bass_kernel_spmd(nc, [arrays], core_ids=[0])
    return r.results[0]["out_0"].reshape(B, T, D)
```

```python
import numpy as np
import concourse.bass as bass
from concourse import mybir
from contextlib import ExitStack

F32 = mybir.dt.float32
F32R = mybir.dt.float32r
BF16 = mybir.dt.bfloat16
I32 = mybir.dt.int32
ALU = mybir.AluOpType
ACT = mybir.ActivationFunctionType
AX_X = mybir.AxisListType.X

B, T, D = 64, 32, 256
NS, R = 8, 16
H, G, HD = 8, 4, 32
BLOCK, NBLK = 16, 257
NPHYS = 16 * NBLK
WINDOW = 128
KEYS = WINDOW + T
FF = 1024
P = 128
QB = P // T
NQ = B // QB
SQ = 4
NSUP = NQ // SQ
ST = SQ * P
NF = FF // P
KV = 2 * G * HD
NTOK = B * T
SCALE = 256.0 ** -0.5
EPS = 1e-6
NEG = -1e30
HALF = HD // 2
WSLOT = 3
TWN = WINDOW // BLOCK + WSLOT
NW = B * WSLOT
CBIG = 70000.0
WROW = 2 * T + 1

W_G, W_U, W_D, W_AD = 0, 2 * FF, 4 * FF, 4 * FF + NF * D
W_AG = W_AD + NF * P
W_AU = W_AG + 2 * P
W_BG = W_AU + 2 * P
W_BU = W_BG + FF
W_BD = W_BU + FF
WCOLS = W_BD + D
PIECE = WCOLS // NQ

C_ID = 0
C_BLK = C_ID + P
C_N16 = C_BLK + QB
C_C32 = C_N16 + 1
C_EPS = C_C32 + 1
C_INV = C_EPS + 1
C_IOTA = C_INV + HALF
C_B4 = C_IOTA + NBLK
C_Q16 = C_B4 + QB
C_B32 = C_Q16 + NQ
C_ONE = C_B32 + 1
CW = C_ONE + P


def constants():
    c = np.zeros((P, CW), np.float32)
    p = np.arange(P)
    c[:, C_ID:C_ID + P] = np.eye(P)
    c[:, C_BLK:C_BLK + QB] = p[:, None] // T == np.arange(QB)
    c[:, C_N16] = p // R
    c[:, C_C32] = p % T
    c[:, C_EPS] = EPS
    c[:, C_INV:C_INV + HALF] = (1.0 / 10000.0 ** (np.arange(HALF, dtype=np.float32) / HALF)).astype(np.float32)
    c[:, C_IOTA:C_IOTA + NBLK] = np.arange(NBLK)
    c[:, C_B4:C_B4 + QB] = p[:, None] % QB == np.arange(QB)
    c[:, C_Q16:C_Q16 + NQ] = p[:, None] // QB == np.arange(NQ)
    c[:, C_B32] = T * p
    c[:, C_ONE:C_ONE + P] = 1.0
    return c


def mask_constants(bf16):
    t, r, q = np.arange(T), np.arange(KEYS), np.arange(P)
    allowed = (r[None, :] > t[:, None]) & (r[None, :] <= WINDOW + t[:, None])
    window = np.where(allowed, 0.0, NEG).astype(bf16)
    pick = np.concatenate([(q[None, :] % T == t[:, None]), np.ones((1, P))]).astype(bf16)
    return window, pick


def two_pi_parts():
    c1 = np.float32(6.28125)
    c2 = np.float32(np.round((2 * np.pi - float(c1)) * 2.0 ** 21) / 2.0 ** 21)
    c3 = np.float32(2 * np.pi - float(c1) - float(c2))
    return float(c1), float(c2), float(c3)


def wait(eng, sem, value):
    if isinstance(value, int) and value <= 0:
        return
    eng.wait_ge(sem, value)


def build(nc, x, wl, wqkv, wo, wmlp, scales, kvpool, subj, subjq, kvlen, kvlenq, table,
          consts, window, pick, out, knew, valid):
    ctx = ExitStack()
    with ctx:
        def sem(name):
            return ctx.enter_context(nc.semaphore(name))

        slab_bytes = 212832
        base = -(-nc.sbuf_base // 32) * 32
        ctx.enter_context(nc.sbuf_tensor("SLAB", [P, slab_bytes // 4], F32))
        at = [0, 0]

        def sb(name, shape, dt=F32):
            size = int(np.prod(shape[1:])) * (2 if dt == BF16 else 4)
            place = at[0]
            at[0] += -(-size // 32) * 32
            at[1] = max(at[1], at[0])
            assert at[1] <= slab_bytes, (name, at)
            return nc.alloc_sbuf_tensor_at(name, shape, dt, offset=base + place)

        XT = sb("XT", [P, 2, NTOK])
        QT = sb("QT", [P, 2, NTOK])
        WH = sb("WH", [P, WCOLS], F32R)
        WR = sb("WR", [P, WCOLS], F32R)
        C = sb("C", [P, CW])
        WO = sb("WO", [P, 2, D])
        LMASK = sb("LMASK", [P, B])
        KEYS_ = sb("KEYALL", [P, NQ + 4, QB + 1])
        WLHC = sb("WLHC", [P, 3, NW])
        PICK = sb("PICK", [T + 1, P], BF16)
        MASK = [sb(f"MASK_{i}", [T + 1, QB, KEYS], BF16) for i in range(2)]
        CM = sb("CM", [P, 4, QB + 1])
        OIDX = [sb(f"OIDX_{i}", [P, QB], I32) for i in range(SQ)]
        NIDX = [sb(f"NIDX_{i}", [P, QB + 1], I32) for i in range(SQ)]
        GATE = sb("GATE", [P, 1])
        WIDX = sb("WIDX", [P, NQ], I32)
        KVM = sb("KVM", [B, KEYS], BF16)
        KV0 = [sb(f"KV0_{i}", [P, QB, KV]) for i in range(2)]
        KV1 = [sb(f"KV1_{i}", [P, KV]) for i in range(2)]
        shared = at[0]

        X = sb("X", [P, NQ, D])
        WL = sb("WL", [P, NQ, WROW])
        WQKV = sb("WQKV", [P, 2, 4 * P])
        TCS = sb("TCS", [P, 2, NQ, 2, HD])
        TC, TS = TCS[:, 0], TCS[:, 1]
        RAW = [sb(f"RAW_{i}", [P, PIECE]) for i in range(SQ)]
        BD0 = [sb(f"BD0_{i}", [P, QB, T]) for i in range(2)]
        BD1 = [sb(f"BD1_{i}", [P, QB, T]) for i in range(2)]
        BDT = [sb(f"BDT_{i}", [P, QB, T]) for i in range(2)]
        X1 = [sb(f"X1_{i}", [P, D]) for i in range(2)]
        X2S = [sb(f"X2S_{i}", [P, 2, P]) for i in range(2)]
        SS = [sb(f"SS_{i}", [P, 3, 12]) for i in range(SQ)]
        setup = at[0]
        SQR = [sb(f"SQR_{i}", [P, 12, HD]) for i in range(2)]
        RA = [sb(f"RA_{i}", [P, 12, HD]) for i in range(2)]
        RB = [sb(f"RB_{i}", [P, 12, HD]) for i in range(2)]
        RS_ = [sb(f"RSUM_{i}", [P, 12, HD]) for i in range(2)]
        QR = [sb(f"QR_{i}", [P, 8, HD]) for i in range(SQ)]
        KVN = [sb(f"KVN_{i}", [P, KV]) for i in range(SQ)]
        at[0] = setup
        SUBI = sb("SUBI", [P, B], I32)
        SUBT = sb("SUBT", [P, NQ], I32)
        ROWF = sb("ROWF", [P, NQ])
        KVT = sb("KVT", [P, NQ], I32)
        KVI = sb("KVI", [B, 1], I32)
        SLOTI = sb("SLOTI", [B, 2], I32)
        SLOTF = sb("SLOTF", [B, 2])
        TABI = sb("TABI", [B, NBLK], I32)
        TABF = sb("TABF", [B, NBLK])
        TSCR = sb("TSCR", [B, 2, NBLK])
        SJ = sb("SJ", [B, TWN])
        TW = sb("TW", [B, TWN])
        TW16 = sb("TW16", [B, TWN])
        KA = sb("KA", [B, TWN, BLOCK])
        OH = sb("OH", [B, BLOCK])
        KEYT = sb("KEYT", [B, 2, KEYS])
        K1E = sb("K1E", [B, QB, T])
        LHC = sb("LHC", [B, 3, WSLOT])
        LHCE = sb("LHCE", [B, 3, WSLOT, B])
        THR = sb("THR", [B, 1])
        POS = sb("POS", [P, NQ])
        ANG = sb("ANG", [P, NQ, HALF])
        TR = sb("TR", [P, 2, 2, NQ, HALF])
        TRG, TRK = TR[:, 0], TR[:, 1]
        SCL = sb("SCL", [P, 2, HD])
        ONE = sb("ONE", [P, 2, HD])

        at[0] = shared
        QBD = [sb(f"QBD_{i}", [P, QB, 2, P]) for i in range(2)]
        KT = sb("KT", [P, QB, KEYS])
        MX = sb("MX", [P, QB, 2])
        NB = sb("NB", [P, QB, 2])
        RSUM = sb("RSM", [P, QB, 2])
        RINV = sb("RINV", [P, QB, 2])
        PE_ = sb("PEXP", [P, QB, 2, KEYS])
        PR0 = sb("PR0", [P, QB, 2, P])
        PR1 = sb("PR1", [P, 2, QB, T])
        PT0 = sb("PT0", [P, QB, 2, P])
        PT1 = sb("PT1", [P, 2, P])
        V1M = [sb(f"V1M_{i}", [P, QB, P]) for i in range(2)]
        OT = sb("OT", [P, 2, QB, T])
        U1 = sb("U1", [P, QB + 1, NW])
        U2 = sb("U2", [P, QB + 1, NW])
        XH = sb("XH", [P, 2, ST], F32R)
        XR = sb("XR", [P, 2, ST], F32R)
        ZH = [sb(f"ZH_{i}", [P, ST], F32R) for i in range(3)]
        ZR = [sb(f"ZR_{i}", [P, ST], F32R) for i in range(3)]
        THGA = sb("THGA", [P, 2, ST])
        TH, GA = THGA[:, 0, :], THGA[:, 1, :]
        X4 = THGA
        HF = sb("HF", [P, ST])
        ZF = [TH, HF[:]]
        HH = [sb(f"HH_{i}", [P, ST], F32R) for i in range(2)]
        HR = [sb(f"HR_{i}", [P, ST], F32R) for i in range(2)]
        OUTB = sb("OUTB", [P, SQ, D])

        PS = ctx.enter_context(nc.psum_tensor("PS", [P, 8, 512], F32))
        ring = PS[:, 5:8, :]

        def cc(at, n=1, rows=P):
            return C[0:rows, at:at + n]

        s_rows, s_tab, s_xfirst, s_xrest, s_wqkv, s_wo_load = (sem(n) for n in ("s_rows", "s_tab", "s_xfirst", "s_xrest", "s_wqkv", "s_wo_load"))
        s_raw = [sem(f"s_raw{i}") for i in range(SQ)]
        s_set = sem("s_set")
        s_widx = sem("s_widx")
        s_wl = [sem("s_wl0"), sem("s_wl1")]
        s_kvm = sem("s_kvm")
        s_kvd = sem("s_kvd")
        s_mask = sem("s_mask")
        s_row = [sem("s_row0"), sem("s_row1")]
        s_keyt, s_lhce, s_keyps, s_keysb = (sem(n) for n in ("s_keyt", "s_lhce", "s_keyps", "s_keysb"))
        s_arg, s_trg = sem("s_arg"), sem("s_trg")
        s_bdt, s_bd, s_l0, s_x1, s_l1, s_x2, s_qkv = (sem(n) for n in ("s_bdt", "s_bd", "s_l0", "s_x1", "s_l1", "s_x2", "s_qkv"))
        s_sq, s_ss, s_rt, s_ab, s_ri, s_rs, s_rot, s_vc = (sem(n) for n in ("s_sq", "s_ss", "s_rt", "s_ab", "s_ri", "s_rs", "s_rot", "s_vc"))
        s_kst = [sem(f"s_kst{i}") for i in range(SQ)]
        s_qt, s_qts = sem("s_qt"), sem("s_qts")
        s_wh, s_wr = sem("s_wh"), sem("s_wr")
        s_zero = sem("s_zero")
        s_m1, s_m2, s_m3, s_m4 = (sem(n) for n in ("s_m1", "s_m2", "s_m3", "s_m4"))
        s_oidx, s_nidx, s_gate = sem("s_oidx"), sem("s_nidx"), sem("s_gate")
        s_old = [sem(f"s_old{i}") for i in range(2)]
        s_new = [sem(f"s_new{i}") for i in range(2)]
        s_vm, s_qbd = sem("s_vm"), sem("s_qbd")
        s_ktp, s_kts = sem("s_ktp"), sem("s_kts")
        s_sc, s_mx, s_nb, s_ex, s_rinv, s_pr = (sem(n) for n in ("s_sc", "s_mx", "s_nb", "s_ex", "s_rinv", "s_pr"))
        s_ptp, s_pta, s_ptd = sem("s_ptp"), sem("s_pta"), sem("s_ptd")
        s_av, s_ot, s_wo, s_x3 = (sem(n) for n in ("s_av", "s_ot", "s_wo", "s_x3"))
        s_xh, s_xr = sem("s_xh"), sem("s_xr")
        s_la, s_zf, s_zh, s_zr = (sem(n) for n in ("s_la", "s_zf", "s_zh", "s_zr"))
        s_g, s_u, s_th, s_ga, s_hf, s_hh, s_hr, s_dn = (sem(n) for n in ("s_g", "s_u", "s_th", "s_ga", "s_hf", "s_hh", "s_hr", "s_dn"))
        s_y, s_x4, s_yt, s_ob, s_out = (sem(n) for n in ("s_y", "s_x4", "s_yt", "s_ob", "s_out"))

        block = ctx.enter_context(nc.Block())

        def phase_a(step, last, eng):
            for u in range(SQ):
                step(0, u)
            with eng.Fori(1, NQ // SQ) as it:
                for u in range(SQ):
                    step(it, u)
            for k in range(NQ, last + 1):
                step(k // SQ, k % SQ)

        def has(n):
            return not isinstance(n, int) or 0 <= n < NQ

        def phase_b(step, eng):
            for u in range(SQ):
                step(0, u, True, False)
            with eng.Fori(1, NSUP) as it:
                for u in range(SQ):
                    step(it, u, True, True)
            for u in range(SQ):
                step(NSUP, u, False, True)

        def uses(it, u, n):
            return (it * 2 + u // 2 + 1) * 16 * n

        @block.sync
        def _(sp):
            for j in range(QB):
                rows = slice(T * j, T * j + T)
                sp.dma_start(SUBT[rows, :], subjq[j:j + 1, :].broadcast_to([T, NQ])).then_inc(s_rows, 16)
            sp.dma_start(TABI[:], table).then_inc(s_tab, 16)
            sp.dma_start(X[:, 0:SQ, :], x[0:ST, :].rearrange("(n p) d -> p n d", p=P)).then_inc(s_xfirst, 16)
            sp.dma_start(WQKV[:], wqkv).then_inc(s_wqkv, 16)
            sp.dma_start(X[:, SQ:NQ, :], x[ST:NTOK, :].rearrange("(n p) d -> p n d", p=P)).then_inc(s_xrest, 16)
            sp.dma_start(WO[:], wo).then_inc(s_wo_load, 16)
            sp.dma_start(PICK[:], pick).then_inc(s_mask, 16)
            for i in range(2):
                sp.dma_start(MASK[i][0:T, :, :], window.rearrange("t (o r) -> t o r", o=1).broadcast_to([T, QB, KEYS])).then_inc(s_mask, 16)

            def load_piece(it, u):
                n = it * SQ + u
                wait(sp, s_wh, n - SQ + 1)
                wait(sp, s_wr, n - SQ + 1)
                sp.dma_start(RAW[u][:], wmlp[:, bass.ds(n * PIECE, PIECE)]).then_inc(s_raw[u], 16)

            def store_new(it, u):
                n = it * SQ + u
                wait(sp, s_rot, n + 1)
                wait(sp, s_vc, n + 1)
                sp.dma_start(knew[bass.ds(n * P, P), :], KVN[u][:]).then_inc(s_kst[u], 16)

            for u in range(SQ):
                load_piece(0, u)
            sp.wait_ge(s_kvm, 1)
            sp.dma_start(valid, KVM[:]).then_inc(s_kvd, 16)
            with sp.Fori(1, NQ // SQ) as it:
                for u in range(SQ):
                    load_piece(it, u)
                    store_new(it - 1, u)
            for u in range(SQ):
                store_new(NQ // SQ - 1, u)

            sp.wait_ge(s_kvd, 16)

            def valid_row(it, u):
                k = it * SQ + u
                wait(sp, s_sc, QB * (k - 1))
                sp.dma_start(MASK[u % 2][T:T + 1, :, :], valid[bass.ds(k * QB, QB), :]).then_inc(s_row[u % 2], 16)

            def store_out(S):
                wait(sp, s_ob, 2 * S + 2)
                sp.dma_start(out[bass.ds(S * ST, ST), :].rearrange("(n p) d -> p n d", p=P), OUTB[:]).then_inc(s_out, 16)

            for u in range(SQ):
                valid_row(0, u)
            for u in range(SQ):
                valid_row(1, u)
            with sp.Fori(2, NSUP) as it:
                for u in range(SQ):
                    valid_row(it, u)
                    if u == 1:
                        store_out(it - 2)
            store_out(NSUP - 2)
            store_out(NSUP - 1)
            sp.wait_ge(s_out, 16 * NSUP)

        @block.gpsimd
        def _(pool):
            nc.gpsimd.memset(KEYS_[:], 0.0).then_inc(s_zero, 1)
            pool.wait_ge(s_widx, 1)
            for n in range(NQ):
                nc.gpsimd.indirect_dma_start(WL[:, n, :], None, wl, bass.IndirectOffsetOnAxis(WIDX[:, n:n + 1], 0)).then_inc(s_wl[n >= SQ], 16)

            def tile(it, u):
                n = it * SQ + u
                i = u % 2
                wait(pool, s_raw[u], 16 * (it + 1))
                wait(pool, s_wh, n + 1)
                cols = bass.ds(n * PIECE, PIECE)
                nc.gpsimd.tensor_tensor(WR[:, cols], RAW[u][:], WH[:, cols].bitcast(F32), ALU.subtract).then_inc(s_wr, 1)
                wait(pool, s_rs, n + 1)
                wait(pool, s_ri, n + 1)
                wait(pool, s_qt, n - SQ + 1)
                if not isinstance(it, int) or it > 0:
                    pool.wait_ge(s_kst[u], it * 16)
                inv = SS[u][:, 2, :]
                nc.gpsimd.tensor_tensor(QR[u][:], RS_[i][:, 0:8, :], inv[:, 0:8].unsqueeze(2).broadcast_to([P, 8, HD]), ALU.mult)
                nc.gpsimd.tensor_tensor(KVN[u][:, 0:P].rearrange("p (h d) -> p h d", h=G), RS_[i][:, 8:12, :],
                                        inv[:, 8:12].unsqueeze(2).broadcast_to([P, G, HD]), ALU.mult).then_inc(s_rot, 1)

            for u in range(SQ):
                tile(0, u)
            with pool.Fori(1, NQ // SQ) as it:
                for u in range(SQ):
                    tile(it, u)

            def gate(passed):
                wait(pool, s_gate, passed)
                nc.gpsimd.tensor_tensor(GATE[:], cc(C_EPS), cc(C_EPS), ALU.add).then_inc(s_gate, 1)

            def old(it, u):
                k = it * SQ + u
                wait(pool, s_oidx, k + 1)
                wait(pool, s_av, k - 1)
                gate(2 * k)
                for j in range(QB):
                    nc.gpsimd.indirect_dma_start(KV0[u % 2][:, j, :], None, kvpool,
                                                 bass.IndirectOffsetOnAxis(OIDX[u][:, j:j + 1], 0)).then_inc(s_old[u % 2], 16)

            def new(it, u):
                k = it * SQ + u
                wait(pool, s_nidx, k + 1)
                wait(pool, s_vm, k - 1)
                wait(pool, s_old[u % 2], uses(it, u, QB))
                gate(2 * k + 1)
                for j in range(QB):
                    nc.gpsimd.indirect_dma_start(KV0[u % 2][:, j, :], None, knew, bass.IndirectOffsetOnAxis(NIDX[u][:, j:j + 1], 0),
                                                 bounds_check=NTOK - 1, oob_is_err=False).then_inc(s_new[u % 2], 16)
                nc.gpsimd.indirect_dma_start(KV1[u % 2][:], None, knew, bass.IndirectOffsetOnAxis(NIDX[u][:, QB:QB + 1], 0)).then_inc(s_new[u % 2], 16)

            def spread_q(it, u):
                k = it * SQ + u
                wait(pool, s_sc, QB * (k - 1))
                wait(pool, s_qts, k + 1)
                for b in range(QB):
                    src = QT[:, :, bass.ds(k * P + b * T, T)].unsqueeze(1).broadcast_to([P, G, 2, T])
                    nc.gpsimd.tensor_tensor(QBD[u % 2][:, b, :, :].rearrange("p c (g h t) -> p (c g) h t", g=2, h=2), src,
                                            cc(C_BLK, G).unsqueeze(2).unsqueeze(3).broadcast_to([P, G, 2, T]), ALU.mult).then_inc(s_qbd, 1)

            def part_v(it, u):
                k = it * SQ + u
                wait(pool, s_new[u % 2], uses(it, u, QB + 1))
                wait(pool, s_av, k - 1)
                nc.gpsimd.tensor_tensor(V1M[u % 2][:], KV1[u % 2][:, P:KV].unsqueeze(1).broadcast_to([P, QB, P]),
                                        cc(C_BLK, QB).unsqueeze(2).broadcast_to([P, QB, P]), ALU.mult).then_inc(s_vm, 1)

            old(0, 0)
            for i in range(SQ):
                pool.wait_ge(s_kst[i], 16 * NQ // SQ)
            pool.wait_ge(s_qts, NQ)
            spread_q(0, 0)
            new(0, 0)
            for u in range(1, SQ):
                part_v(0, u - 1)
                old(0, u)
                spread_q(0, u)
                new(0, u)
            with pool.Fori(1, NSUP) as it:
                for u in range(SQ):
                    part_v(it if u else it - 1, (u - 1) % SQ)
                    old(it, u)
                    spread_q(it, u)
                    new(it, u)
            part_v(NSUP - 1, SQ - 1)

        @block.scalar
        def _(act):
            act.dma_start(C[:], consts).then_inc(s_rows, 16)
            for j in range(QB):
                rows = slice(T * j, T * j + T)
                act.dma_start(KVT[rows, :], kvlenq[j:j + 1, :].broadcast_to([T, NQ])).then_inc(s_tab, 16)
            act.dma_start(SCL[:].rearrange("p a d -> p (a d)"), scales.rearrange("(o n) -> o n", o=1).broadcast_to([P, 2 * HD])).then_inc(s_tab, 16)
            act.dma_start(KVI[:], kvlen.rearrange("(b o) -> b o", o=1)).then_inc(s_tab, 16)
            act.dma_start(SUBI[:], subj.rearrange("(o b) -> o b", o=1).broadcast_to([P, B])).then_inc(s_tab, 16)
            act.wait_ge(s_arg, 1)
            nc.scalar.activation(TRG, TRK, ACT.Sin).then_inc(s_trg, 1)

            def step_a(it, u):
                k = it * SQ + u
                n, i = k - 1, (u - 1) % 2
                if has(n):
                    wait(act, s_l1, n + 1)
                    wait(act, s_qkv, n - 1)
                    src = PS[:, 2 + i, 0:D].rearrange("p (h t) -> p h t", h=2)
                    nc.scalar.activation(X2S[i][:], src, ACT.Copy)
                    nc.scalar.activation(XT[:, :, bass.ds(n * P, P)], src, ACT.Copy).then_inc(s_x2, 1)
                if has(k):
                    wait(act, s_raw[u], 16 * (it + 1))
                    nc.scalar.activation(WH[:, bass.ds(k * PIECE, PIECE)], RAW[u][:], ACT.Copy).then_inc(s_wh, 1)
                n = k - 3
                if has(n):
                    v = (u - 3) % SQ
                    wait(act, s_ss, n + 1)
                    nc.scalar.activation(SS[v][:, 1, :], SS[v][:, 0, :], ACT.Sqrt, bias=cc(C_EPS), scale=1.0 / HD).then_inc(s_rt, 1)
                n, i, v = k - 2, u % 2, (u - 2) % SQ
                if has(n):
                    wait(act, s_qkv, n + 1)
                    wait(act, s_ss, n - 1)
                    nc.scalar.activation(SQR[i][:], PS[:, 4 + i, 0:12 * HD].rearrange("p (h d) -> p h d", h=12), ACT.Square).then_inc(s_sq, 1)
                    wait(act, s_kst[v], 16 * (it if u >= 2 else it - 1))
                    nc.scalar.activation(KVN[v][:, P:KV], PS[:, 4 + i, 12 * HD:16 * HD], ACT.Copy).then_inc(s_vc, 1)
                n = k - 4
                if has(n):
                    wait(act, s_qt, n + 1)
                    nc.scalar.activation(QT[:, :, bass.ds(n * P, P)], PS[:, 6 + u % 2, 0:D].rearrange("p (h t) -> p h t", h=2), ACT.Copy).then_inc(s_qts, 1)

            phase_a(step_a, NQ + 3, act)

            def tanh(F):
                wait(act, s_g, F + 1)
                wait(act, s_ga, F)
                nc.scalar.activation(TH, PS[:, 0, :], ACT.Tanh, scale=0.5).then_inc(s_th, 1)

            def high_h(F, f, first):
                wait(act, s_hf, F + 1)
                if not first:
                    wait(act, s_dn, F - 1)
                nc.scalar.activation(HH[f % 2][:], HF[:], ACT.Copy).then_inc(s_hh, 1)

            def high_x(k, at, n):
                nc.scalar.activation(XH[:, :, P * at:P * (at + n)], XT[:, :, bass.ds(k * P, P * n)], ACT.Copy).then_inc(s_xh, 1)

            def step_b(it, u, attn, mlp):
                k = it * SQ + u
                S = it - 1
                F = S * NF + 2 * u

                def keys_t():
                    wait(act, s_ktp, 2 * k + 1)
                    wait(act, s_sc, QB * k)
                    nc.scalar.activation(KT[:, :, 0:P], ring[:, 0, :].rearrange("p (b r) -> p b r", b=QB), ACT.Copy)
                    wait(act, s_ktp, 2 * k + 2)
                    nc.scalar.activation(KT[:, :, P:KEYS], ring[:, 1, 0:P].rearrange("p (b r) -> p b r", b=QB), ACT.Copy).then_inc(s_kts, 1)

                def exps():
                    for b in range(QB):
                        wait(act, s_nb, QB * k + b + 1)
                        if b == 0:
                            wait(act, s_pr, k)
                        for gp in range(2):
                            nc.scalar.activation(PE_[:, b, gp, :], ring[:, b % 3, KEYS * gp:KEYS * gp + KEYS], ACT.Exp,
                                                 bias=NB[:, b, gp:gp + 1], scale=SCALE,
                                                 accum_out=RSUM[:, b, gp:gp + 1]).then_inc(s_ex, 1)

                def probs_t():
                    for j in range(2):
                        wait(act, s_ptp, 3 * k + j + 1)
                        if j == 0:
                            wait(act, s_av, k)
                        nc.scalar.activation(PT0[:, 2 * j:2 * j + 2, :, :].rearrange("p b g q -> p (b g q)"), ring[:, 1 + j, :], ACT.Copy).then_inc(s_pta, 1)

                def outputs_t():
                    for j in range(2):
                        wait(act, s_yt, 2 * S + j + 1)
                        wait(act, s_out, 16 * S)
                        nc.scalar.activation(OUTB[:, 2 * j:2 * j + 2, :].rearrange("p n d -> p (n d)"), PS[:, j, :], ACT.Copy).then_inc(s_ob, 1)

                def heads_t():
                    wait(act, s_av, k + 1)
                    wait(act, s_wo, k)
                    nc.scalar.activation(OT[:].rearrange("p h b t -> p b h t"), ring[:, 2, 0:D].rearrange("p (b h t) -> p b h t", b=QB, h=2), ACT.Copy).then_inc(s_ot, 1)

                if attn:
                    keys_t()
                if mlp and u == 0:
                    for j in range(2):
                        wait(act, s_zf, 3 * S + j + 1)
                        nc.scalar.activation(ZH[j][:], ZF[j], ACT.Copy).then_inc(s_zh, 1)
                if u == 0 and attn:
                    exps()
                if mlp:
                    tanh(F)
                    high_h(F, 0, u == 0)
                if u > 0 and attn:
                    exps()
                if mlp and u > 0:
                    tanh(F + 1)
                if attn:
                    probs_t()
                if mlp and u == 0:
                    tanh(F + 1)
                if mlp:
                    high_h(F + 1, 1, False)
                if u == SQ - 1 and attn:
                    if mlp:
                        wait(act, s_u, NF * S + NF)
                    wait(act, s_x3, SQ * it + SQ - 1)
                    high_x(k - (SQ - 1), 0, SQ - 1)
                if attn:
                    heads_t()
                if u == SQ - 1 and mlp:
                    wait(act, s_zf, 3 * S + 3)
                    nc.scalar.activation(ZH[2][:], ZF[0], ACT.Copy).then_inc(s_zh, 1)
                if u == SQ - 1 and attn:
                    wait(act, s_x3, SQ * it + SQ)
                    high_x(k, SQ - 1, 1)
                if u == SQ - 1 and mlp:
                    outputs_t()

            phase_b(step_b, act)

        @block.vector
        def _(dve):
            done = [0]

            def link(ins):
                done[0] += 1
                ins.then_inc(s_set, 1)
                dve.wait_ge(s_set, done[0])

            v = nc.vector
            dve.wait_ge(s_rows, 16 * (QB + 1))
            link(v.tensor_scalar(ROWF[:], SUBT[:], float(T), cc(C_C32), ALU.mult, ALU.add))
            v.tensor_copy(WIDX[:], ROWF[:]).then_inc(s_widx, 1)
            dve.wait_ge(s_tab, 16 * (QB + 4))
            v.tensor_scalar(LMASK[:], SUBI[:], cc(C_N16), None, ALU.is_equal)
            v.tensor_scalar(SLOTI[:, 0:1], KVI[:], 4, None, ALU.logical_shift_right)
            v.tensor_scalar(SLOTI[:, 1:2], KVI[:], 15, None, ALU.bitwise_and)
            v.tensor_copy(TABF[:], TABI[:])
            link(v.tensor_scalar(THR[:], KVI[:], -1.0, float(WINDOW), ALU.mult, ALU.add))
            v.tensor_scalar(KVM[:], cc(C_IOTA, KEYS, B), THR[:, 0:1], NEG, ALU.is_lt, ALU.mult).then_inc(s_kvm, 1)
            link(v.tensor_copy(SLOTF[:], SLOTI[:]))
            v.tensor_scalar(OH[:], cc(C_IOTA, BLOCK, B), SLOTF[:, 1:2], None, ALU.is_equal)
            link(v.tensor_scalar(SJ[:], cc(C_IOTA, TWN, B), SLOTF[:, 0:1], float(-(WINDOW // BLOCK)), ALU.add, ALU.add))
            for j in range(TWN):
                link(v.scalar_tensor_tensor(TSCR[:, j % 2, :], cc(C_IOTA, NBLK, B), SJ[:, j:j + 1], TABF[:], ALU.is_equal, ALU.mult,
                                            accum_out=TW[:, j:j + 1]))
            link(v.tensor_scalar(TW16[:], TW[:], float(BLOCK), None, ALU.mult))
            link(v.tensor_tensor(KA[:], TW16[:].unsqueeze(2).broadcast_to([B, TWN, BLOCK]),
                                 cc(C_IOTA, BLOCK, B).unsqueeze(1).broadcast_to([B, TWN, BLOCK]), ALU.add))
            kaf = KA[:].rearrange("b j o -> b (j o)")
            link(v.tensor_scalar(KEYT[:, 0, :], kaf[:, 0:KEYS], OH[:, 0:1], None, ALU.mult))
            for m in range(1, BLOCK):
                link(v.scalar_tensor_tensor(KEYT[:, m % 2, :], kaf[:, m:m + KEYS], OH[:, m:m + 1], KEYT[:, (m - 1) % 2, :], ALU.mult, ALU.add))
            keyt = KEYT[:, (BLOCK - 1) % 2, :]
            v.tensor_tensor(K1E[:], keyt[:, P:KEYS].unsqueeze(1).broadcast_to([B, QB, T]),
                            cc(C_B4, QB, B).unsqueeze(2).broadcast_to([B, QB, T]), ALU.mult).then_inc(s_keyt, 1)
            rem = SLOTF[:, 1:2]
            last = TW16[:, TWN - WSLOT:TWN]
            v.tensor_copy(LHC[:, 0, 1:3], last[:, 1:3])
            v.tensor_scalar(LHC[:, 0, 0:1], last[:, 0:1], rem, None, ALU.add)
            v.tensor_scalar(LHC[:, 1, 0:2], last[:, 0:2], float(BLOCK - 1), None, ALU.add)
            v.tensor_scalar(LHC[:, 1, 2:3], last[:, 2:3], rem, -1.0, ALU.add, ALU.add)
            link(v.tensor_scalar(LHC[:, 2, :], last, -1.0, rem, ALU.mult, ALU.subtract))
            link(v.scalar_tensor_tensor(TSCR[:, 0, 0:WSLOT], cc(C_IOTA, WSLOT, B), float(BLOCK), LHC[:, 2, :], ALU.mult, ALU.add))
            link(v.tensor_scalar(LHC[:, 2, :], TSCR[:, 0, 0:WSLOT], cc(C_B32, 1, B), CBIG, ALU.add, ALU.add))
            v.tensor_tensor(LHCE[:].rearrange("b x i c -> b (x i) c"),
                            LHC[:].rearrange("b x i -> b (x i)").unsqueeze(2).broadcast_to([B, 3 * WSLOT, B]),
                            cc(C_ID, B, B).unsqueeze(1).broadcast_to([B, 3 * WSLOT, B]), ALU.mult).then_inc(s_lhce, 1)
            dve.wait_ge(s_keyps, 4)
            dve.wait_ge(s_zero, 1)
            v.tensor_copy(KEYS_[:, 0:NQ, 0:QB], PS[:, 7, 0:B].rearrange("p (n j) -> p n j", j=QB))
            v.tensor_copy(KEYS_[:, 0:NQ, QB], PS[:, 7, B:B + NQ])
            v.tensor_copy(WLHC[:, 0:2, :].rearrange("p x w -> p (x w)"), PS[:, 6, 0:2 * NW])
            v.tensor_copy(WLHC[:, 2, :], PS[:, 5, 0:NW]).then_inc(s_keysb, 1)
            dve.wait_ge(s_keysb, 1)

            link(v.tensor_scalar(POS[:], KVT[:], cc(C_C32), None, ALU.add))
            link(v.tensor_tensor(ANG[:], POS[:].unsqueeze(2).broadcast_to([P, NQ, HALF]),
                                 cc(C_INV, HALF).unsqueeze(1).broadcast_to([P, NQ, HALF]), ALU.mult))
            magic = 1.5 * 2.0 ** 23
            c1, c2, c3 = two_pi_parts()
            v.tensor_scalar(TRG[:, 0], ANG[:], 1.0 / (2 * np.pi), 0.25, ALU.mult, ALU.add)
            link(v.tensor_scalar(TRG[:, 1], ANG[:], 1.0 / (2 * np.pi), None, ALU.mult))
            link(v.tensor_scalar(TRK[:], TRG[:], magic, None, ALU.add))
            link(v.tensor_scalar(TRG[:], TRK[:], -magic, None, ALU.add))
            for i in range(2):
                link(v.scalar_tensor_tensor(TRK[:, i], TRG[:, i], -c1, ANG[:], ALU.mult, ALU.add))
            trg, trk = (t[:].rearrange("p a n f -> p (a n f)") for t in (TRG, TRK))
            link(v.scalar_tensor_tensor(trk, trg, -c2, trk, ALU.mult, ALU.add))
            link(v.scalar_tensor_tensor(trk, trg, -c3, trk, ALU.mult, ALU.add))
            link(v.tensor_scalar(TRK[:, 0], TRK[:, 0], float(np.pi / 2), None, ALU.add))
            v.tensor_scalar(TRK[:], TRK[:], 3.1415925, -3.1415925, ALU.min, ALU.max).then_inc(s_arg, 1)
            link(v.tensor_scalar(ONE[:], SCL[:], 1.0, None, ALU.add))
            dve.wait_ge(s_trg, 1)
            for a in range(2):
                for h in range(2):
                    hs, other = slice(HALF * h, HALF * h + HALF), slice(HALF * (1 - h), HALF * (1 - h) + HALF)
                    v.tensor_tensor(TC[:, :, a, hs], TRG[:, 0], ONE[:, a, hs].unsqueeze(1).broadcast_to([P, NQ, HALF]), ALU.mult)
                    link(v.tensor_tensor(TS[:, :, a, hs], TRG[:, 1], ONE[:, a, other].unsqueeze(1).broadcast_to([P, NQ, HALF]), ALU.mult))
            link(v.tensor_scalar(TS[:, :, :, 0:HALF], TS[:, :, :, 0:HALF], -1.0, None, ALU.mult))

            def blocks(n, i):
                wait(dve, s_l0, n - 1)
                wait(dve, s_l1, n - 1)
                mask = cc(C_BLK, QB).unsqueeze(2).broadcast_to([P, QB, T])
                w = WL[:, bass.ds(n, 1), :].rearrange("p o c -> p (o c)")
                v.tensor_tensor(BDT[i][:], w[:, T:2 * T].unsqueeze(1).broadcast_to([P, QB, T]), mask, ALU.mult).then_inc(s_bdt, 1)
                v.tensor_tensor(BD0[i][:], w[:, 0:T].unsqueeze(1).broadcast_to([P, QB, T]), mask, ALU.mult)
                wait(dve, s_bdt, n + 1)
                v.tensor_tensor(BD1[i][:], BDT[i][:], cc(C_ID, P).rearrange("p (j c) -> p j c", j=QB), ALU.add).then_inc(s_bd, 1)

            def step_a(it, u):
                k = it * SQ + u
                if has(k):
                    blocks(k, u % 2)
                n, i = k - 1, (u - 1) % 2
                if has(n):
                    wait(dve, s_l0, n + 1)
                    wait(dve, s_l1, n - 1)
                    v.scalar_tensor_tensor(X1[i][:], PS[:, i, 0:D], WL[:, bass.ds(n, 1), 2 * T:2 * T + 1].rearrange("p o c -> p (o c)"),
                                           X[:, bass.ds(n, 1), :].rearrange("p o d -> p (o d)"), ALU.add, ALU.add).then_inc(s_x1, 1)
                n, i, s = k - 3, (u - 3) % 2, (u - 3) % SQ
                if has(n):
                    wait(dve, s_sq, n + 1)
                    v.reduce_sum(SS[s][:, 0, :], SQR[i][:], AX_X).then_inc(s_ss, 1)
                    wait(dve, s_vc, n + 1)
                    qk = PS[:, 4 + i, 0:12 * HD].rearrange("p (h d) -> p h d", h=12)
                    tc = TC[:, bass.ds(n, 1), :, :].rearrange("p o a d -> p (o a) d")
                    ts = TS[:, bass.ds(n, 1), :, :].rearrange("p o a d -> p (o a) d")
                    for a, lo, hi in ((0, 0, 8), (1, 8, 12)):
                        m = hi - lo
                        v.tensor_tensor(RA[i][:, lo:hi, :], qk[:, lo:hi, :], tc[:, a:a + 1, :].broadcast_to([P, m, HD]), ALU.mult)
                        for h in range(2):
                            hs, other = slice(HALF * h, HALF * h + HALF), slice(HALF * (1 - h), HALF * (1 - h) + HALF)
                            last = v.tensor_tensor(RB[i][:, lo:hi, hs], qk[:, lo:hi, other], ts[:, a:a + 1, hs].broadcast_to([P, m, HALF]), ALU.mult)
                    last.then_inc(s_ab, 1)
                    wait(dve, s_ab, n + 1)
                    wait(dve, s_rot, n - 1)
                    v.tensor_tensor(RS_[i][:], RA[i][:], RB[i][:], ALU.add).then_inc(s_rs, 1)
                    wait(dve, s_rt, n + 1)
                    v.reciprocal(SS[s][:, 2, :], SS[s][:, 1, :]).then_inc(s_ri, 1)

            dve.wait_ge(s_wl[0], 16 * SQ)
            dve.wait_ge(s_xfirst, 16)
            for u in range(SQ):
                step_a(0, u)
            dve.wait_ge(s_wl[1], 16 * (NQ - SQ))
            dve.wait_ge(s_xrest, 16)
            with dve.Fori(1, NQ // SQ) as it:
                for u in range(SQ):
                    step_a(it, u)
            for u in range(3):
                step_a(NQ // SQ, u)

            def match(it, u):
                k = it * SQ + u
                wait(dve, s_nidx, k)
                for j in range(QB + 1):
                    key = KEYS_[:, bass.ds(k, 1), j:j + 1].rearrange("p o c -> p (o c)")
                    v.scalar_tensor_tensor(U1[:, j, :], WLHC[:, 0, :], key, WLHC[:, 2, :], ALU.is_le, ALU.mult).then_inc(s_m1, 1)
                wait(dve, s_old[u % 2], uses(it - 1, u, QB))
                v.tensor_scalar(OIDX[u][:], KEYS_[:, bass.ds(k, 1), 0:QB].rearrange("p o c -> p (o c)"), 0.0, None, ALU.add).then_inc(s_oidx, 1)
                for j in range(QB + 1):
                    key = KEYS_[:, bass.ds(k, 1), j:j + 1].rearrange("p o c -> p (o c)")
                    wait(dve, s_m1, (QB + 1) * k + j + 1)
                    last = v.scalar_tensor_tensor(U2[:, j, :], WLHC[:, 1, :], key, U1[:, j, :], ALU.is_ge, ALU.mult)
                last.then_inc(s_m2, 1)
                wait(dve, s_m2, k + 1)
                v.tensor_reduce(CM[:, 0, :], U2[:], AX_X, ALU.max).then_inc(s_m3, 1)
                wait(dve, s_m3, k + 1)
                v.tensor_scalar(CM[:, 1, :], CM[:, 0, :], 0.0, 4.0 * CBIG, ALU.is_equal, ALU.mult)
                v.tensor_tensor(CM[:, 2, :], CM[:, 0, :], KEYS_[:, bass.ds(k, 1), :].rearrange("p o c -> p (o c)"), ALU.add).then_inc(s_m4, 1)
                wait(dve, s_m4, k + 1)
                wait(dve, s_new[u % 2], uses(it - 1, u, QB + 1))
                v.scalar_tensor_tensor(NIDX[u][:], CM[:, 2, :], -CBIG, CM[:, 1, :], ALU.add, ALU.add).then_inc(s_nidx, 1)

            def gated(F, f, first):
                wait(dve, s_th, F + 1)
                v.scalar_tensor_tensor(GA, TH, 1.0, PS[:, 0, :], ALU.add, ALU.mult).then_inc(s_ga, 1)
                wait(dve, s_ga, F + 1)
                wait(dve, s_u, F + 1)
                wait(dve, s_hh, F)
                v.scalar_tensor_tensor(HF[:], PS[:, 1, :], 0.5, GA, ALU.mult, ALU.mult).then_inc(s_hf, 1)

            def rest_h(F, f, first):
                wait(dve, s_hh, F + 1)
                if not first:
                    wait(dve, s_dn, F - 1)
                v.tensor_tensor(HR[f % 2][:], HF[:], HH[f % 2][:].bitcast(F32), ALU.subtract).then_inc(s_hr, 1)

            def own_adapter(S, j, bank, z):
                wait(dve, s_zh, 3 * S + (2 if j == 2 else 0))
                own = LMASK[:, bass.ds(S * QB * SQ, QB * SQ)].unsqueeze(2).broadcast_to([P, QB * SQ, T])
                v.tensor_tensor(z.rearrange("p (b t) -> p b t", t=T), PS[:, bank, :].rearrange("p (b t) -> p b t", t=T),
                                own, ALU.mult).then_inc(s_zf, 1)

            def rest_z(S, j, z):
                wait(dve, s_zh, 3 * S + j + 1)
                v.tensor_tensor(ZR[j][:], z, ZH[j][:].bitcast(F32), ALU.subtract).then_inc(s_zr, 1)

            def rest_x(k, at, n):
                cols = slice(P * at, P * (at + n))
                v.tensor_tensor(XR[:, :, cols], XT[:, :, bass.ds(k * P, P * n)], XH[:, :, cols].bitcast(F32), ALU.subtract).then_inc(s_xr, 1)

            def add_attention(k):
                wait(dve, s_wo, k + 1)
                xq = XT[:, :, bass.ds(k * P, P)]
                v.tensor_tensor(xq, ring[:, 2, 0:2 * P].rearrange("p (h t) -> p h t", h=2), xq, ALU.add).then_inc(s_x3, 1)

            def step_b(it, u, attn, mlp):
                k = it * SQ + u
                S = it - 1
                F = S * NF + 2 * u

                def maxima():
                    for b in range(QB):
                        wait(dve, s_sc, QB * k + b + 1)
                        if b == 0:
                            wait(dve, s_ex, 2 * QB * k)
                        v.reduce_max(MX[:, b, :], ring[:, b % 3, 0:2 * KEYS].rearrange("p (g r) -> p g r", g=2), AX_X).then_inc(s_mx, 1)
                        wait(dve, s_mx, QB * k + b + 1)
                        v.tensor_scalar(NB[:, b, :], MX[:, b, :], -SCALE, None, ALU.mult).then_inc(s_nb, 1)

                def normalise():
                    wait(dve, s_ex, 2 * QB * (k + 1))
                    v.reciprocal(RINV[:].rearrange("p b g -> p (b g)"), RSUM[:].rearrange("p b g -> p (b g)")).then_inc(s_rinv, 1)
                    wait(dve, s_rinv, k + 1)
                    wait(dve, s_ptp, 3 * k)
                    for b in range(QB):
                        for gp in range(2):
                            v.tensor_scalar(PR0[:, b, gp, :], PE_[:, b, gp, 0:P], RINV[:, b, gp:gp + 1], None, ALU.mult)
                    v.tensor_tensor(PR1[:], PE_[:, :, :, P:KEYS].rearrange("p b g r -> p g b r"),
                                    RINV[:].rearrange("p b g -> p g b").unsqueeze(3).broadcast_to([P, 2, QB, T]), ALU.mult).then_inc(s_pr, 1)

                if mlp and u == 0:
                    wait(dve, s_la, 2 * S + 1)
                    own_adapter(S, 0, 4, ZF[0])
                    wait(dve, s_la, 2 * S + 2)
                    own_adapter(S, 1, 2, ZF[1])
                    rest_z(S, 0, ZF[0])
                    rest_z(S, 1, ZF[1])
                if u == 0 and attn:
                    maxima()
                    normalise()
                if mlp:
                    gated(F, 0, u == 0)
                if u > 0 and attn:
                    add_attention(k - 1)
                if mlp:
                    rest_h(F, 0, u == 0)
                if u > 0 and attn:
                    maxima()
                    normalise()
                if mlp:
                    gated(F + 1, 1, False)
                if attn:
                    wait(dve, s_av, k)
                    wait(dve, s_ptp, 3 * k + 3)
                    v.tensor_copy(PT1[:].rearrange("p g q -> p (g q)"), ring[:, 0, 0:2 * P]).then_inc(s_ptd, 1)
                if mlp:
                    rest_h(F + 1, 1, False)
                if u == SQ - 1 and attn:
                    wait(dve, s_xh, 2 * it + 1)
                    rest_x(k - (SQ - 1), 0, SQ - 1)
                if u == SQ - 1 and mlp:
                    wait(dve, s_dn, NF * S + NF)
                    own_adapter(S, 2, 4, ZF[0])
                    rest_z(S, 2, ZF[0])
                if u == SQ - 1 and attn:
                    add_attention(k)
                if u == SQ - 1 and mlp:
                    wait(dve, s_y, S + 1)
                    wait(dve, s_yt, 2 * S)
                    v.tensor_tensor(X4[:], PS[:, 2:4, :], XT[:, :, bass.ds(S * ST, ST)], ALU.add).then_inc(s_x4, 1)
                if u == SQ - 1 and attn:
                    wait(dve, s_xh, 2 * it + 2)
                    rest_x(k, SQ - 1, 1)
                if attn:
                    match(it + (u + 2) // SQ, (u + 2) % SQ)

            dve.wait_ge(s_wr, NQ)
            match(0, 0)
            match(0, 1)
            phase_b(step_b, dve)

        @block.tensor
        def _(pe):
            mm = nc.tensor.matmul
            ident = cc(C_ID, P)

            def tr(o, i):
                return nc.tensor.transpose(o, i, ident[0:i.shape[0], 0:i.shape[0]])

            def mm3(o, at, high, rest, start, stop):
                wh, wr = WH[:, at:at + P], WR[:, at:at + P]
                mm(o, wh, high, start=start, stop=False)
                mm(o, wh, rest, start=False, stop=False)
                return mm(o, wr, high, start=False, stop=stop)

            pe.wait_ge(s_rows, 16 * (QB + 1))
            keyt = KEYT[:, (BLOCK - 1) % 2, :]
            pe.wait_ge(s_keyt, 1)
            tr(PS[:, 7, 0:B], keyt[:, 0:P]).then_inc(s_keyps, 1)
            mm(PS[:, 7, B:B + NQ], K1E[:].rearrange("b j t -> b (j t)"), cc(C_Q16, NQ, B), start=True, stop=True).then_inc(s_keyps, 1)
            pe.wait_ge(s_lhce, 1)
            e = LHCE[:].rearrange("b x i c -> b (x i c)")
            mm(PS[:, 6, 0:2 * NW], cc(C_ONE, P, B), e[:, 0:2 * NW], start=True, stop=True).then_inc(s_keyps, 1)
            mm(PS[:, 5, 0:NW], cc(C_ONE, P, B), e[:, 2 * NW:3 * NW], start=True, stop=True).then_inc(s_keyps, 1)

            pe.wait_ge(s_xfirst, 16)
            pe.wait_ge(s_wqkv, 16)
            pe.wait_ge(s_keysb, 1)

            def step_a(it, u):
                k = it * SQ + u
                if has(k):
                    wait(pe, s_bd, k + 1)
                    wait(pe, s_x1, k - 1)
                    mm(PS[:, u % 2, 0:D], BD0[u % 2][:].rearrange("p j c -> p (j c)"), X[:, bass.ds(k, 1), :], start=True, stop=True).then_inc(s_l0, 1)
                n, i = k - 1, (u - 1) % 2
                if has(n):
                    wait(pe, s_x1, n + 1)
                    wait(pe, s_x2, n - 1)
                    for h in range(2):
                        last = mm(PS[:, 2 + i, P * h:P * h + P], X1[i][:, P * h:P * h + P], BD1[i][:].rearrange("p j c -> p (j c)"), start=True, stop=True)
                    last.then_inc(s_l1, 1)
                n, i = k - 2, u % 2
                if has(n):
                    wait(pe, s_x2, n + 1)
                    wait(pe, s_ab, n - 1)
                    wait(pe, s_vc, n - 1)
                    for h in range(2):
                        last = mm(PS[:, 4 + i, :], X2S[i][:, h, :], WQKV[:, h, :], start=h == 0, stop=h == 1)
                    last.then_inc(s_qkv, 1)
                n = k - 4
                if has(n):
                    wait(pe, s_rot, n + 1)
                    wait(pe, s_qts, n)
                    for h in range(2):
                        last = tr(PS[:, 6 + u % 2, P * h:P * h + P], QR[u][:, G * h:G * h + G, :].rearrange("p h d -> p (h d)"))
                    last.then_inc(s_qt, 1)

            phase_a(step_a, NQ + 3, pe)
            pe.wait_ge(s_qts, NQ)
            pe.wait_ge(s_ab, NQ)
            pe.wait_ge(s_vc, NQ)
            pe.wait_ge(s_x2, NQ)
            pe.wait_ge(s_mask, 48)
            pe.wait_ge(s_wo_load, 16)
            pe.wait_ge(s_wr, NQ)

            def low_rank(S):
                wait(pe, s_xr, 2 * (S + 1))
                wait(pe, s_zf, 3 * S)
                wait(pe, s_x4, S)
                for bank, at in ((4, W_AG), (2, W_AU)):
                    for h in range(2):
                        last = mm3(PS[:, bank, :], at + P * h, XH[:, h, :], XR[:, h, :], h == 0, h == 1)
                    last.then_inc(s_la, 1)

            def up(S, f):
                F = S * NF + f
                wait(pe, s_ga, F)
                if f == 0:
                    wait(pe, s_ob, 2 * S)
                for h in range(2):
                    mm3(PS[:, 0, :], W_G + FF * h + P * f, XH[:, h, :], XR[:, h, :], h == 0, False)
                if f > 0:
                    mm3(PS[:, 0, :], W_BG + P * f, ZH[0][:], ZR[0][:], False, True).then_inc(s_g, 1)
                wait(pe, s_hf, F)
                for h in range(2):
                    mm3(PS[:, 1, :], W_U + FF * h + P * f, XH[:, h, :], XR[:, h, :], h == 0, False)
                if f == 0:
                    wait(pe, s_zr, 3 * S + 2)
                    mm3(PS[:, 0, :], W_BG + P * f, ZH[0][:], ZR[0][:], False, True).then_inc(s_g, 1)
                mm3(PS[:, 1, :], W_BU + P * f, ZH[1][:], ZR[1][:], False, True).then_inc(s_u, 1)

            def down(S, f):
                wait(pe, s_hr, S * NF + f + 1)
                if f == 0:
                    wait(pe, s_zf, 3 * S + 2)
                for h in range(2):
                    mm3(PS[:, 2 + h, :], W_D + D * f + P * h, HH[f % 2][:], HR[f % 2][:], f == 0, False)
                mm3(PS[:, 4, :], W_AD + P * f, HH[f % 2][:], HR[f % 2][:], f == 0, f == NF - 1).then_inc(s_dn, 1)

            def output_proj(k):
                wait(pe, s_ot, k + 1)
                for h in range(2):
                    for hl in range(2):
                        last = mm(ring[:, 2, P * h:P * h + P], WO[:, hl, P * h:P * h + P], OT[:, hl, :, :].rearrange("p b t -> p (b t)"),
                                  start=hl == 0, stop=hl == 1)
                last.then_inc(s_wo, 1)

            def step_b(it, u, attn, mlp):
                k = it * SQ + u
                S = it - 1

                def keys_t():
                    wait(pe, s_new[u % 2], uses(it, u, QB + 1))
                    for b in range(QB):
                        last = tr(ring[:, 0, P * b:P * b + P], KV0[u % 2][:, b, 0:P])
                    last.then_inc(s_ktp, 1)
                    tr(ring[:, 1, 0:P], KV1[u % 2][:, 0:P]).then_inc(s_ktp, 1)

                def scores():
                    wait(pe, s_kts, k + 1)
                    wait(pe, s_qbd, G * (k + 1))
                    wait(pe, s_row[u % 2], uses(it, u, 1))
                    for b in range(QB):
                        if b == 2:
                            wait(pe, s_x3, k)
                        if b == 3:
                            wait(pe, s_ex, 2 * QB * k + 2)
                        for gp in range(2):
                            o = ring[:, b % 3, KEYS * gp:KEYS * gp + KEYS]
                            mm(o, QBD[u % 2][:, b, gp, :], KT[:, b, :], start=True, stop=False)
                            last = mm(o, PICK[:], MASK[u % 2][:, b, :], start=False, stop=True)
                        last.then_inc(s_sc, 1)

                def probs_t():
                    wait(pe, s_pr, k + 1)
                    for b in range(QB):
                        for gp in range(2):
                            j = 2 * b + gp
                            last = tr(ring[:, 1 + j // 4, P * (j % 4):P * (j % 4) + P], PR0[:, b, gp, :])
                        if b % 2:
                            last.then_inc(s_ptp, 1)
                    for gp in range(2):
                        last = tr(ring[:, 0, P * gp:P * gp + P], PR1[:, gp, :, :].rearrange("p b r -> p (b r)"))
                    last.then_inc(s_ptp, 1)

                def weigh_v():
                    wait(pe, s_ptd, k + 1)
                    wait(pe, s_pta, 2 * k + 2)
                    wait(pe, s_vm, k + 1)
                    for b in range(QB):
                        for start in (True, False):
                            for g in range(G):
                                rows, qs = slice(HD * g, HD * g + HD), slice(64 * (g % 2), 64 * (g % 2) + 64)
                                o = ring[rows, 2, 64 * b:64 * b + 64]
                                if start:
                                    mm(o, KV0[u % 2][:, b, P + HD * g:P + HD * g + HD], PT0[:, b, g // 2, qs], start=True, stop=False)
                                else:
                                    last = mm(o, V1M[u % 2][:, b, HD * g:HD * g + HD], PT1[:, g // 2, qs], start=False, stop=True)
                    last.then_inc(s_av, 1)

                if attn:
                    keys_t()
                if u == 0:
                    if mlp:
                        low_rank(S)
                    if attn:
                        scores()
                    if mlp:
                        up(S, 0)
                    if attn:
                        probs_t()
                    if mlp:
                        up(S, 1)
                    if attn:
                        weigh_v()
                    if mlp:
                        down(S, 0)
                    return
                if mlp:
                    up(S, 2 * u)
                if attn:
                    output_proj(k - 1)
                if mlp:
                    down(S, 2 * u - 1)
                if attn:
                    scores()
                if mlp:
                    up(S, 2 * u + 1)
                if attn:
                    probs_t()
                if mlp:
                    down(S, 2 * u)
                if attn:
                    weigh_v()
                if u == SQ - 1 and mlp:
                    down(S, NF - 1)
                if u == SQ - 1 and attn:
                    output_proj(k)
                if u == SQ - 1 and mlp:
                    wait(pe, s_zr, 3 * S + 3)
                    for h in range(2):
                        last = mm3(PS[:, 2 + h, :], W_BD + P * h, ZH[2][:], ZR[2][:], False, True)
                    last.then_inc(s_y, 1)
                    wait(pe, s_x4, S + 1)
                    for j in range(2):
                        for n in range(2):
                            for h in range(2):
                                last = tr(PS[:, j, D * n + P * h:D * n + P * h + P], X4[:, h, P * (2 * j + n):P * (2 * j + n) + P])
                        last.then_inc(s_yt, 1)

            phase_b(step_b, pe)


def kernel(x, itok_B_0_7, fside_8xS_0, itok_Bx257_0_4111, itok_B_37_3939, L0_cond_weights, L1_cond_weights,
           L2_cond_Wq, L2_cond_Wk, L2_cond_Wv, L2_cond_Wo, L2_cond_q_norm_scale, L2_cond_k_norm_scale,
           L2_cond_k_blocks, L2_cond_v_blocks, L3_cond_Wg, L3_cond_Wu, L3_cond_Wd, L3_cond_Ag, L3_cond_Bg,
           L3_cond_Au, L3_cond_Bu, L3_cond_Ad, L3_cond_Bd):
    import ml_dtypes
    import concourse.bacc as bacc
    from concourse.bass_utils import run_bass_kernel_spmd

    def lay(a, *shape):
        return np.ascontiguousarray(np.asarray(a).reshape(shape))

    def flip(a, *order):
        return np.ascontiguousarray(np.transpose(np.asarray(a), order))

    wq = flip(lay(L2_cond_Wq, G, 2, HD, D), 3, 1, 0, 2).reshape(D, P * 2)
    wk, wv = flip(L2_cond_Wk, 1, 0), flip(L2_cond_Wv, 1, 0)
    wqkv = flip(np.concatenate([wq, wk, wv], 1).reshape(2, P, 4 * P), 1, 0, 2)
    wo = flip(lay(L2_cond_Wo, D, G, 2, HD), 1, 3, 2, 0).reshape(P, 2, D)

    def rows(w, n):
        return flip(lay(w, n, P, -1), 1, 0, 2)

    def low(a, n):
        return rows(flip(a, 1, 0, 2).reshape(n * P, P), n)

    kvpool = np.concatenate([flip(L2_cond_k_blocks, 0, 2, 1, 3).reshape(NPHYS * BLOCK, P),
                             flip(L2_cond_v_blocks, 0, 2, 1, 3).reshape(NPHYS * BLOCK, P)], 1)
    wl = np.concatenate([lay(L0_cond_weights, NS * T, T), lay(L1_cond_weights, NS * T, T), lay(fside_8xS_0, NS * T, 1)], 1)
    wmlp = np.concatenate([lay(w, P, -1) for w in (
        rows(L3_cond_Wg, 2), rows(L3_cond_Wu, 2), rows(L3_cond_Wd, NF), low(L3_cond_Ad, NF), low(L3_cond_Ag, 2),
        low(L3_cond_Au, 2), L3_cond_Bg, L3_cond_Bu, L3_cond_Bd)], 1)
    window, pick = mask_constants(ml_dtypes.bfloat16)
    arrays = {
        "x": lay(x, NTOK, D), "wl": wl, "wqkv": wqkv, "wo": wo, "wmlp": wmlp,
        "scales": np.concatenate([np.asarray(L2_cond_q_norm_scale), np.asarray(L2_cond_k_norm_scale)]),
        "kvpool": kvpool, "subj": lay(itok_B_0_7, B), "subjq": flip(lay(itok_B_0_7, NQ, QB), 1, 0),
        "kvlen": lay(itok_B_37_3939, B), "kvlenq": flip(lay(itok_B_37_3939, NQ, QB), 1, 0),
        "table": lay(itok_Bx257_0_4111, B, NBLK),
        "consts": constants(), "window": window, "pick": pick,
    }
    nc = bacc.Bacc("TRN2", target_bir_lowering=False, num_devices=1)
    arrays = {f"in_{n}": a for n, a in arrays.items()}
    args = [nc.dram_tensor(n, a.shape, mybir.dt.from_np(a.dtype), kind="ExternalInput").ap() for n, a in arrays.items()]
    out = nc.dram_tensor("out_0", (NTOK, D), F32, kind="ExternalOutput").ap()
    knew = nc.dram_tensor("k_new", (NTOK, KV), F32).ap()
    valid = nc.dram_tensor("key_valid", (B, KEYS), BF16).ap()
    build(nc, *args, out, knew, valid)
    r = run_bass_kernel_spmd(nc, [arrays], core_ids=[0])
    return r.results[0]["out_0"].reshape(B, T, D)
```

```python
import numpy as np
import concourse.bass as bass
from concourse import mybir
from contextlib import ExitStack

F32 = mybir.dt.float32
F32R = mybir.dt.float32r
BF16 = mybir.dt.bfloat16
I32 = mybir.dt.int32
ALU = mybir.AluOpType
ACT = mybir.ActivationFunctionType
AX_X = mybir.AxisListType.X

B, T, D = 64, 32, 256
NS, R = 8, 16
H, G, HD = 8, 4, 32
BLOCK, NBLK = 16, 257
NPHYS = 16 * NBLK
WINDOW = 128
KEYS = WINDOW + T
FF = 1024
P = 128
QB = P // T
NQ = B // QB
SQ = 4
NSUP = NQ // SQ
ST = SQ * P
NF = FF // P
KV = 2 * G * HD
NTOK = B * T
SCALE = 256.0 ** -0.5
EPS = 1e-6
NEG = -1e30
HALF = HD // 2
WSLOT = 3
TWN = WINDOW // BLOCK + WSLOT
NW = B * WSLOT
CBIG = 70000.0
WROW = 2 * T + 1

W_G, W_U, W_D, W_AD = 0, 2 * FF, 4 * FF, 4 * FF + NF * D
W_AG = W_AD + NF * P
W_AU = W_AG + 2 * P
W_BG = W_AU + 2 * P
W_BU = W_BG + FF
W_BD = W_BU + FF
WCOLS = W_BD + D
PIECE = WCOLS // NQ

C_ID = 0
C_BLK = C_ID + P
C_N16 = C_BLK + QB
C_C32 = C_N16 + 1
C_EPS = C_C32 + 1
C_INV = C_EPS + 1
C_IOTA = C_INV + HALF
C_B4 = C_IOTA + NBLK
C_Q16 = C_B4 + QB
C_B32 = C_Q16 + NQ
C_ONE = C_B32 + 1
CW = C_ONE + P


def constants():
    c = np.zeros((P, CW), np.float32)
    p = np.arange(P)
    c[:, C_ID:C_ID + P] = np.eye(P)
    c[:, C_BLK:C_BLK + QB] = p[:, None] // T == np.arange(QB)
    c[:, C_N16] = p // R
    c[:, C_C32] = p % T
    c[:, C_EPS] = EPS
    c[:, C_INV:C_INV + HALF] = (1.0 / 10000.0 ** (np.arange(HALF, dtype=np.float32) / HALF)).astype(np.float32)
    c[:, C_IOTA:C_IOTA + NBLK] = np.arange(NBLK)
    c[:, C_B4:C_B4 + QB] = p[:, None] % QB == np.arange(QB)
    c[:, C_Q16:C_Q16 + NQ] = p[:, None] // QB == np.arange(NQ)
    c[:, C_B32] = T * p
    c[:, C_ONE:C_ONE + P] = 1.0
    return c


def mask_constants(bf16):
    t, r, q = np.arange(T), np.arange(KEYS), np.arange(P)
    allowed = (r[None, :] > t[:, None]) & (r[None, :] <= WINDOW + t[:, None])
    window = np.where(allowed, 0.0, NEG).astype(bf16)
    pick = np.concatenate([(q[None, :] % T == t[:, None]), np.ones((1, P))]).astype(bf16)
    return window, pick


def two_pi_parts():
    c1 = np.float32(6.28125)
    c2 = np.float32(np.round((2 * np.pi - float(c1)) * 2.0 ** 21) / 2.0 ** 21)
    c3 = np.float32(2 * np.pi - float(c1) - float(c2))
    return float(c1), float(c2), float(c3)


def build(nc, x, wl, wqkv, wo, wmlp, scales, kvpool, subj, kvlen, perpart, table,
          consts, window, pick, out, knew, valid):
    ctx = ExitStack()
    with ctx:
        def sem(name):
            return ctx.enter_context(nc.semaphore(name))

        slab_bytes = 212832
        base = -(-nc.sbuf_base // 32) * 32
        ctx.enter_context(nc.sbuf_tensor("SLAB", [P, slab_bytes // 4], F32))
        at = [0, 0]

        def sb(name, shape, dt=F32):
            size = int(np.prod(shape[1:])) * (2 if dt == BF16 else 4)
            place = at[0]
            at[0] += -(-size // 32) * 32
            at[1] = max(at[1], at[0])
            assert at[1] <= slab_bytes, (name, at)
            return nc.alloc_sbuf_tensor_at(name, shape, dt, offset=base + place)

        XT = sb("XT", [P, 2, NTOK])
        QT = sb("QT", [P, 2, NTOK])
        WH = sb("WH", [P, WCOLS], F32R)
        WR = sb("WR", [P, WCOLS], F32R)
        C = sb("C", [P, CW])
        WO = sb("WO", [P, 2, D])
        LMASK = sb("LMASK", [P, B])
        KEYS_ = sb("KEYALL", [P, NQ + 4, QB + 1])
        WLHC = sb("WLHC", [P, 3, NW])
        PICK = sb("PICK", [T + 1, P], BF16)
        MASK = [sb(f"MASK_{i}", [T + 1, QB, KEYS], BF16) for i in range(2)]
        CM = sb("CM", [P, 4, QB + 1])
        OIDX = [sb(f"OIDX_{i}", [P, QB], I32) for i in range(SQ)]
        NIDX = [sb(f"NIDX_{i}", [P, QB + 1], I32) for i in range(SQ)]
        GATE = sb("GATE", [P, 1])
        WIDX = sb("WIDX", [P, NQ], I32)
        STARTED = sb("STARTED", [P, 18])
        KVM = sb("KVM", [B, KEYS], BF16)
        KV0 = [sb(f"KV0_{i}", [P, QB, KV]) for i in range(SQ)]
        KV1 = [sb(f"KV1_{i}", [P, KV]) for i in range(2)]
        shared = at[0]

        X = sb("X", [P, NQ, D])
        WL = sb("WL", [P, NQ, WROW])
        WQKV = sb("WQKV", [P, 2, 4 * P])
        TCS = sb("TCS", [P, 2, NQ, 2, HD])
        TC, TS = TCS[:, 0], TCS[:, 1]
        RAW = [sb(f"RAW_{i}", [P, PIECE]) for i in range(SQ)]
        BD0 = [sb(f"BD0_{i}", [P, QB, T]) for i in range(2)]
        BD1 = [sb(f"BD1_{i}", [P, QB, T]) for i in range(2)]
        BDT = sb("BDT", [P, QB, T])
        X1 = [sb(f"X1_{i}", [P, D]) for i in range(2)]
        X2S = [sb(f"X2S_{i}", [P, 2, P]) for i in range(2)]
        SS = [sb(f"SS_{i}", [P, 3, 12]) for i in range(SQ)]
        setup = at[0]
        SQR = [sb(f"SQR_{i}", [P, 12, HD]) for i in range(2)]
        RA = [sb(f"RA_{i}", [P, 12, HD]) for i in range(2)]
        RB = [sb(f"RB_{i}", [P, 12, HD]) for i in range(2)]
        RS_ = [sb(f"RSUM_{i}", [P, 12, HD]) for i in range(2)]
        QR = [sb(f"QR_{i}", [P, 8, HD]) for i in range(SQ)]
        KVN = [sb(f"KVN_{i}", [P, KV]) for i in range(SQ)]
        at[0] = setup
        SUBI = sb("SUBI", [P, B], I32)
        SKT = sb("SKT", [P, 2, NQ], I32)
        SUBT, KVT = SKT[:, 0, :], SKT[:, 1, :]
        ROWF = sb("ROWF", [P, NQ])
        KVI = sb("KVI", [B, 1], I32)
        SLOTI = sb("SLOTI", [B, 2], I32)
        SLOTF = sb("SLOTF", [B, 2])
        TABI = sb("TABI", [B, NBLK], I32)
        TABF = sb("TABF", [B, NBLK])
        TSCR = sb("TSCR", [B, 2, NBLK])
        SJ = sb("SJ", [B, TWN])
        TW = sb("TW", [B, TWN])
        TW16 = sb("TW16", [B, TWN])
        KA = sb("KA", [B, TWN, BLOCK])
        BITI = sb("BITI", [B, 4], I32)
        BITF = sb("BITF", [B, 4])
        KDIF = sb("KDIF", [B, KEYS + BLOCK // 2])
        K1E = sb("K1E", [B, QB, T])
        LHC = sb("LHC", [B, 3, WSLOT])
        LHCE = sb("LHCE", [B, 3, WSLOT, B])
        THR = sb("THR", [B, 1])
        POS = sb("POS", [P, NQ])
        ANG = sb("ANG", [P, NQ, HALF])
        TR = sb("TR", [P, 2, 2, NQ, HALF])
        TRG, TRK = TR[:, 0], TR[:, 1]
        SCL = sb("SCL", [P, 2, HD])
        ONE = sb("ONE", [P, 2, 2, HD])

        at[0] = shared
        U = sb("U", [P, QB + 1, NW])
        QBD = [sb(f"QBD_{i}", [P, QB, 2, P]) for i in range(2)]
        KT = sb("KT", [P, QB, KEYS])
        MX = sb("MX", [P, QB, 2])
        NB = sb("NB", [P, QB, 2])
        RSUM = sb("RSM", [P, QB, 2])
        RINV = sb("RINV", [P, QB, 2])
        PE_ = sb("PEXP", [P, QB, 2, KEYS])
        PR1 = sb("PR1", [P, 2, QB, T])
        PT0 = sb("PT0", [P, QB, 2, P])
        PT1 = sb("PT1", [P, 2, P])
        V1M = [sb(f"V1M_{i}", [P, QB, P]) for i in range(2)]
        OT = sb("OT", [P, 2, QB, T])
        XH = sb("XH", [P, 2, ST], F32R)
        XR = sb("XR", [P, 2, ST], F32R)
        ZH = [sb(f"ZH_{i}", [P, ST], F32R) for i in range(3)]
        ZR = [sb(f"ZR_{i}", [P, ST], F32R) for i in range(3)]
        THGA = sb("THGA", [P, 2, ST])
        TH, GA = THGA[:, 0, :], THGA[:, 1, :]
        X4 = THGA
        HF = sb("HF", [P, ST])
        ZF = [TH, HF[:]]
        HH = [sb(f"HH_{i}", [P, ST], F32R) for i in range(2)]
        HR = [sb(f"HR_{i}", [P, ST], F32R) for i in range(2)]
        OUTB = sb("OUTB", [P, SQ, D])

        PS = ctx.enter_context(nc.psum_tensor("PS", [P, 8, 512], F32))
        ring = PS[:, 5:8, :]

        def cc(at, n=1, rows=P):
            return C[0:rows, at:at + n]

        rows_loaded = sem("rows_loaded")
        tables_loaded = sem("tables_loaded")
        x_first_loaded = sem("x_first_loaded")
        x_rest_loaded = sem("x_rest_loaded")
        wqkv_loaded = sem("wqkv_loaded")
        wo_loaded = sem("wo_loaded")
        piece_loaded = [sem(f"piece_loaded{i}") for i in range(SQ)]
        mask_loaded = sem("mask_loaded")
        valid_loaded = [sem(f"valid_loaded{i}") for i in range(2)]
        subject_rows = [sem(f"subject_rows{i}") for i in range(2)]
        setup_done = sem("setup_done")
        subject_index = sem("subject_index")
        keys_zeroed = sem("keys_zeroed")
        valid_ready = sem("valid_ready")
        valid_stored = sem("valid_stored")
        keys_ready = sem("keys_ready")
        intervals_ready = sem("intervals_ready")
        keys_spread = sem("keys_spread")
        keys_kept = sem("keys_kept")
        angles_ready = sem("angles_ready")
        sines_ready = sem("sines_ready")
        rope_ready = sem("rope_ready")
        w1_blocks = sem("w1_blocks")
        blocks_ready = sem("blocks_ready")
        xw0_ready = sem("xw0_ready")
        x1_ready = sem("x1_ready")
        x2_summed = sem("x2_summed")
        x2_kept = sem("x2_kept")
        qkv_ready = sem("qkv_ready")
        squares_ready = sem("squares_ready")
        square_sums = sem("square_sums")
        roots_ready = sem("roots_ready")
        inverses_ready = sem("inverses_ready")
        rope_parts = sem("rope_parts")
        rotated = sem("rotated")
        q_ready = sem("q_ready")
        k_ready = sem("k_ready")
        v_ready = sem("v_ready")
        new_stored = [sem(f"new_stored{i}") for i in range(SQ)]
        qt_kept = sem("qt_kept")
        qt_summed = sem("qt_summed")
        high_split = sem("high_split")
        rest_split = sem("rest_split")
        low_tested = sem("low_tested")
        high_tested = sem("high_tested")
        code_found = sem("code_found")
        token_found = sem("token_found")
        old_index = sem("old_index")
        new_index = sem("new_index")
        gates_passed = sem("gates_passed")
        old_gathered = [sem(f"old_gathered{i}") for i in range(SQ)]
        new_gathered = [sem(f"new_gathered{i}") for i in range(2)]
        v_parted = sem("v_parted")
        q_spread = sem("q_spread")
        keys_turned = sem("keys_turned")
        keys_taken = sem("keys_taken")
        scores_ready = sem("scores_ready")
        maxima_found = sem("maxima_found")
        bias_ready = sem("bias_ready")
        exps_ready = sem("exps_ready")
        sums_inverted = sem("sums_inverted")
        probs_ready_act = sem("probs_ready_act")
        probs_ready_dve = sem("probs_ready_dve")
        probs_turned = sem("probs_turned")
        probs_taken_act = sem("probs_taken_act")
        probs_taken_dve = sem("probs_taken_dve")
        heads_ready = sem("heads_ready")
        heads_taken = sem("heads_taken")
        attn_ready = sem("attn_ready")
        x3_ready = sem("x3_ready")
        x3_high = sem("x3_high")
        x3_rest = sem("x3_rest")
        low_rank_ready = sem("low_rank_ready")
        own_ready = sem("own_ready")
        own_high = sem("own_high")
        own_rest = sem("own_rest")
        gated_ready = sem("gated_ready")
        gate_ready = sem("gate_ready")
        up_ready = sem("up_ready")
        tanh_ready = sem("tanh_ready")
        h_ready = sem("h_ready")
        h_high = sem("h_high")
        h_rest = sem("h_rest")
        down_added = sem("down_added")
        out_turned = sem("out_turned")
        out_ready = sem("out_ready")
        x4_ready = sem("x4_ready")
        out_taken = sem("out_taken")
        out_stored = sem("out_stored")

        from_one = [gated_ready, down_added, out_stored, own_high, h_high, out_turned, own_ready, x4_ready, out_taken, h_ready, rotated, qt_kept, k_ready, v_ready, *new_stored]
        counts_started = sem("counts_started")

        def wait(eng, semaphore, count):
            if isinstance(count, int) and count <= 0:
                return
            eng.wait_ge(semaphore, count + 1 if any(semaphore is f for f in from_one) else count)

        block = ctx.enter_context(nc.Block())

        def phase_a(step, last, eng):
            for u in range(SQ):
                step(0, u)
            with eng.Fori(1, NQ // SQ) as it:
                for u in range(SQ):
                    step(it, u)
            for k in range(NQ, last + 1):
                step(k // SQ, k % SQ)

        def has(n):
            return not isinstance(n, int) or 0 <= n < NQ

        def phase_b(step, eng):
            for u in range(SQ):
                step(0, u, True, False)
            with eng.Fori(1, NSUP) as it:
                for u in range(SQ):
                    step(it, u, True, True)
            for u in range(SQ):
                step(NSUP, u, False, True)

        def uses(it, u, n):
            return (it * 2 + u // 2 + 1) * 16 * n

        @block.sync
        def _(sp):
            sp.dma_start(SKT[:].rearrange("p a n -> p (a n)"), perpart).then_inc(rows_loaded, 16)
            sp.dma_start(TABI[:], table).then_inc(tables_loaded, 16)
            sp.dma_start(X[:, 0:SQ, :], x[0:ST, :].rearrange("(n p) d -> p n d", p=P)).then_inc(x_first_loaded, 16)
            sp.dma_start(WQKV[:], wqkv).then_inc(wqkv_loaded, 16)
            sp.wait_ge(tables_loaded, 64)
            sp.dma_start(X[:, SQ:NQ, :], x[ST:NTOK, :].rearrange("(n p) d -> p n d", p=P)).then_inc(x_rest_loaded, 16)
            sp.dma_start(WO[:], wo).then_inc(wo_loaded, 16)
            sp.dma_start(PICK[:], pick).then_inc(mask_loaded, 16)
            for i in range(2):
                sp.dma_start(MASK[i][0:T, :, :], window.rearrange("t (o r) -> t o r", o=1).broadcast_to([T, QB, KEYS])).then_inc(mask_loaded, 16)

            def load_piece(it, u):
                n = it * SQ + u
                wait(sp, high_split, n - SQ + 1)
                wait(sp, rest_split, n - SQ + 1)
                sp.dma_start(RAW[u][:], wmlp[:, bass.ds(n * PIECE, PIECE)]).then_inc(piece_loaded[u], 16)

            def store_new(it, u):
                n = it * SQ + u
                wait(sp, k_ready, n + 1)
                wait(sp, v_ready, n + 1)
                sp.dma_start(knew[bass.ds(n * P, P), :], KVN[u][:]).then_inc(new_stored[u], 16)

            sp.wait_ge(counts_started, 1)
            for u in range(SQ):
                load_piece(0, u)
            sp.wait_ge(valid_ready, 1)
            sp.dma_start(valid, KVM[:]).then_inc(valid_stored, 16)
            with sp.Fori(1, NQ // SQ) as it:
                for u in range(SQ):
                    load_piece(it, u)
                    store_new(it - 1, u)
            for u in range(SQ):
                store_new(NQ // SQ - 1, u)

            sp.wait_ge(valid_stored, 16)

            def valid_row(it, u):
                k = it * SQ + u
                wait(sp, scores_ready, QB * (k - 1))
                sp.dma_start(MASK[u % 2][T:T + 1, :, :], valid[bass.ds(k * QB, QB), :]).then_inc(valid_loaded[u % 2], 16)

            def store_out(S):
                wait(sp, out_taken, 2 * S + 2)
                sp.dma_start(out[bass.ds(S * ST, ST), :].rearrange("(n p) d -> p n d", p=P), OUTB[:]).then_inc(out_stored, 16)

            for u in range(SQ):
                valid_row(0, u)
            for u in range(SQ):
                valid_row(1, u)
            with sp.Fori(2, NSUP) as it:
                for u in range(SQ):
                    valid_row(it, u)
                    if u == 1:
                        store_out(it - 2)
            store_out(NSUP - 2)
            store_out(NSUP - 1)
            wait(sp, out_stored, 16 * NSUP)

        @block.gpsimd
        def _(pool):
            for i, one in enumerate(from_one):
                nc.gpsimd.memset(STARTED[:, i:i + 1], 0.0).then_inc(one, 1)
            nc.gpsimd.memset(KEYS_[:], 0.0).then_inc(keys_zeroed, 1)
            nc.gpsimd.memset(GATE[:], 0.0).then_inc(counts_started, 1)
            pool.wait_ge(counts_started, 1)
            pool.wait_ge(subject_index, 1)
            for n in range(NQ):
                nc.gpsimd.indirect_dma_start(WL[:, n, :], None, wl, bass.IndirectOffsetOnAxis(WIDX[:, n:n + 1], 0)).then_inc(subject_rows[n >= SQ], 16)

            def gate(passed):
                wait(pool, gates_passed, passed)
                nc.gpsimd.tensor_tensor(GATE[:], cc(C_EPS), cc(C_EPS), ALU.add).then_inc(gates_passed, 1)

            def old(it, u):
                k = it * SQ + u
                wait(pool, old_index, k + 1)
                wait(pool, heads_ready, k - SQ + 1)
                if not isinstance(k, int) or k >= 1:
                    gate(2 * k - 1)
                for j in range(QB):
                    nc.gpsimd.indirect_dma_start(KV0[u][:, j, :], None, kvpool,
                                                 bass.IndirectOffsetOnAxis(OIDX[u][:, j:j + 1], 0)).then_inc(old_gathered[u], 16)

            pool.wait_ge(sines_ready, 1)
            for a in range(2):
                for h in range(2):
                    hs, other = slice(HALF * h, HALF * h + HALF), slice(HALF * (1 - h), HALF * (1 - h) + HALF)
                    nc.gpsimd.tensor_tensor(TC[:, :, a, hs], TRG[:, 0], ONE[:, 0, a, hs].unsqueeze(1).broadcast_to([P, NQ, HALF]), ALU.mult)
                    last = nc.gpsimd.tensor_tensor(TS[:, :, a, hs], TRG[:, 1], ONE[:, 1 - h, a, other].unsqueeze(1).broadcast_to([P, NQ, HALF]), ALU.mult)
            last.then_inc(rope_ready, 1)
            old(0, 0)

            def tile(it, u):
                n = it * SQ + u
                i = u % 2
                wait(pool, rope_parts, n + 1)
                wait(pool, q_ready, n - 1)
                wait(pool, k_ready, n - 1)
                nc.gpsimd.tensor_tensor(RS_[i][:], RA[i][:], RB[i][:], ALU.add).then_inc(rotated, 1)
                wait(pool, rotated, n + 1)
                wait(pool, inverses_ready, n + 1)
                wait(pool, qt_summed, n - SQ + 1)
                inv = SS[u][:, 2, :]
                nc.gpsimd.tensor_tensor(QR[u][:], RS_[i][:, 0:8, :], inv[:, 0:8].unsqueeze(2).broadcast_to([P, 8, HD]), ALU.mult).then_inc(q_ready, 1)

            def rest_piece(it, u):
                n = it * SQ + u
                wait(pool, piece_loaded[u], 16 * (it + 1))
                wait(pool, high_split, n + 1)
                cols = bass.ds(n * PIECE, PIECE)
                nc.gpsimd.tensor_tensor(WR[:, cols], RAW[u][:], WH[:, cols].bitcast(F32), ALU.subtract).then_inc(rest_split, 1)

            def tiles(it, last=False):
                for u in range(SQ):
                    tile(it, u)
                    if not last or u < 2:
                        rest_piece(it + (u + 2) // SQ, (u + 2) % SQ)

            for u in range(2):
                rest_piece(0, u)
            tiles(0)
            with pool.Fori(1, NQ // SQ - 1) as it:
                tiles(it)
            tiles(NQ // SQ - 1, last=True)

            def new(it, u):
                k = it * SQ + u
                wait(pool, new_index, k + 1)
                wait(pool, v_parted, k - 1)
                wait(pool, old_gathered[u], 16 * QB * (it + 1))
                gate(2 * k)
                for j in range(QB):
                    nc.gpsimd.indirect_dma_start(KV0[u][:, j, :], None, knew, bass.IndirectOffsetOnAxis(NIDX[u][:, j:j + 1], 0),
                                                 bounds_check=NTOK - 1, oob_is_err=False).then_inc(new_gathered[u % 2], 16)
                nc.gpsimd.indirect_dma_start(KV1[u % 2][:], None, knew, bass.IndirectOffsetOnAxis(NIDX[u][:, QB:QB + 1], 0)).then_inc(new_gathered[u % 2], 16)

            def spread_q(it, u):
                k = it * SQ + u
                wait(pool, scores_ready, QB * (k - 1))
                wait(pool, qt_kept, k + 1)
                for b in range(QB):
                    src = QT[:, :, bass.ds(k * P + b * T, T)].unsqueeze(1).broadcast_to([P, G, 2, T])
                    nc.gpsimd.tensor_tensor(QBD[u % 2][:, b, :, :].rearrange("p c (g h t) -> p (c g) h t", g=2, h=2), src,
                                            cc(C_BLK, G).unsqueeze(2).unsqueeze(3).broadcast_to([P, G, 2, T]), ALU.mult).then_inc(q_spread, 1)

            def part_v(it, u):
                k = it * SQ + u
                wait(pool, new_gathered[u % 2], uses(it, u, QB + 1))
                wait(pool, heads_ready, k - 1)
                nc.gpsimd.tensor_tensor(V1M[u % 2][:], KV1[u % 2][:, P:KV].unsqueeze(1).broadcast_to([P, QB, P]),
                                        cc(C_BLK, QB).unsqueeze(2).broadcast_to([P, QB, P]), ALU.mult).then_inc(v_parted, 1)

            wait(pool, qt_kept, NQ)
            spread_q(0, 0)
            for i in range(SQ):
                wait(pool, new_stored[i], 16 * NQ // SQ)
            new(0, 0)
            for u in range(1, SQ):
                old(0, u)
                part_v(0, u - 1)
                spread_q(0, u)
                new(0, u)
            with pool.Fori(1, NSUP) as it:
                for u in range(SQ):
                    old(it, u)
                    part_v(it if u else it - 1, (u - 1) % SQ)
                    spread_q(it, u)
                    new(it, u)
            part_v(NSUP - 1, SQ - 1)

        @block.scalar
        def _(act):
            act.dma_start(C[:], consts).then_inc(rows_loaded, 16)
            act.dma_start(SCL[:].rearrange("p a d -> p (a d)"), scales.rearrange("(o n) -> o n", o=1).broadcast_to([P, 2 * HD])).then_inc(tables_loaded, 16)
            act.dma_start(KVI[:], kvlen.rearrange("(b o) -> b o", o=1)).then_inc(tables_loaded, 16)
            act.dma_start(SUBI[:], subj.rearrange("(o b) -> o b", o=1).broadcast_to([P, B])).then_inc(tables_loaded, 16)
            act.wait_ge(counts_started, 1)
            act.wait_ge(angles_ready, 1)
            nc.scalar.activation(TRG, TRK, ACT.Sin).then_inc(sines_ready, 1)

            def step_a(it, u):
                k = it * SQ + u
                n, i = k - 1, (u - 1) % 2
                if has(n):
                    wait(act, x2_summed, n + 1)
                    wait(act, qkv_ready, n - 1)
                    src = PS[:, 2 + i, 0:D].rearrange("p (h t) -> p h t", h=2)
                    nc.scalar.activation(X2S[i][:], src, ACT.Copy)
                    nc.scalar.activation(XT[:, :, bass.ds(n * P, P)], src, ACT.Copy).then_inc(x2_kept, 1)
                n = k - 3
                if has(n):
                    v = (u - 3) % SQ
                    wait(act, square_sums, n + 1)
                    nc.scalar.activation(SS[v][:, 1, :], SS[v][:, 0, :], ACT.Sqrt, bias=cc(C_EPS), scale=1.0 / HD).then_inc(roots_ready, 1)
                if has(k):
                    wait(act, piece_loaded[u], 16 * (it + 1))
                    nc.scalar.activation(WH[:, bass.ds(k * PIECE, PIECE)], RAW[u][:], ACT.Copy).then_inc(high_split, 1)
                n, i, v = k - 2, u % 2, (u - 2) % SQ
                if has(n):
                    wait(act, qkv_ready, n + 1)
                    wait(act, square_sums, n - 1)
                    nc.scalar.activation(SQR[i][:], PS[:, 4 + i, 0:12 * HD].rearrange("p (h d) -> p h d", h=12), ACT.Square).then_inc(squares_ready, 1)
                    wait(act, new_stored[v], 16 * (it if u >= 2 else it - 1))
                    nc.scalar.activation(KVN[v][:, P:KV], PS[:, 4 + i, 12 * HD:16 * HD], ACT.Copy).then_inc(v_ready, 1)
                n = k - 4
                if has(n):
                    wait(act, qt_summed, n + 1)
                    nc.scalar.activation(QT[:, :, bass.ds(n * P, P)], PS[:, 6 + u % 2, 0:D].rearrange("p (h t) -> p h t", h=2), ACT.Copy).then_inc(qt_kept, 1)

            phase_a(step_a, NQ + 3, act)

            def tanh(F):
                wait(act, gate_ready, F + 1)
                wait(act, gated_ready, F)
                nc.scalar.activation(TH, PS[:, 0, :], ACT.Tanh, scale=0.5).then_inc(tanh_ready, 1)

            def high_h(F, f, first):
                wait(act, h_ready, F + 1)
                if not first:
                    wait(act, down_added, F - 1)
                nc.scalar.activation(HH[f % 2][:], HF[:], ACT.Copy).then_inc(h_high, 1)

            def high_x(k, at, n):
                nc.scalar.activation(XH[:, :, P * at:P * (at + n)], XT[:, :, bass.ds(k * P, P * n)], ACT.Copy).then_inc(x3_high, 1)

            def step_b(it, u, attn, mlp):
                k = it * SQ + u
                S = it - 1
                F = S * NF + 2 * u

                def keys_t():
                    wait(act, keys_turned, 2 * k + 1)
                    wait(act, scores_ready, QB * k)
                    nc.scalar.activation(KT[:, :, 0:P], ring[:, 0, :].rearrange("p (b r) -> p b r", b=QB), ACT.Copy)
                    wait(act, keys_turned, 2 * k + 2)
                    nc.scalar.activation(KT[:, :, P:KEYS], ring[:, 1, 0:P].rearrange("p (b r) -> p b r", b=QB), ACT.Copy).then_inc(keys_taken, 1)

                def exps(first=0, last=QB):
                    for b in range(first, last):
                        wait(act, bias_ready, QB * k + b + 1)
                        if b == 0:
                            wait(act, probs_turned, 3 * k)
                        for gp in range(2):
                            nc.scalar.activation(PE_[:, b, gp, :], ring[:, b % 3, KEYS * gp:KEYS * gp + KEYS], ACT.Exp,
                                                 bias=NB[:, b, gp:gp + 1], scale=SCALE,
                                                 accum_out=RSUM[:, b, gp:gp + 1]).then_inc(exps_ready, 1)

                def normalise():
                    wait(act, sums_inverted, k + 1)
                    for b in range(2, QB):
                        for gp in range(2):
                            last = nc.scalar.activation(PE_[:, b, gp, 0:P], PE_[:, b, gp, 0:P], ACT.Copy, scale=RINV[:, b, gp:gp + 1])
                    last.then_inc(probs_ready_act, 1)

                def probs_t():
                    for j in range(2):
                        wait(act, probs_turned, 3 * k + j + 1)
                        if j == 0:
                            wait(act, heads_ready, k)
                        nc.scalar.activation(PT0[:, 2 * j:2 * j + 2, :, :].rearrange("p b g q -> p (b g q)"), ring[:, 1 + j, :], ACT.Copy).then_inc(probs_taken_act, 1)

                def outputs_t():
                    for j in range(2):
                        wait(act, out_turned, 2 * S + j + 1)
                        wait(act, out_stored, 16 * S)
                        nc.scalar.activation(OUTB[:, 2 * j:2 * j + 2, :].rearrange("p n d -> p (n d)"), PS[:, j, :], ACT.Copy).then_inc(out_taken, 1)

                def heads_t():
                    wait(act, heads_ready, k + 1)
                    wait(act, attn_ready, k)
                    nc.scalar.activation(OT[:].rearrange("p h b t -> p b h t"), ring[:, 2, 0:D].rearrange("p (b h t) -> p b h t", b=QB, h=2), ACT.Copy).then_inc(heads_taken, 1)

                if attn:
                    keys_t()
                if u == 0 and attn:
                    exps(0, 2)
                if mlp and u == 0:
                    for j in range(2):
                        wait(act, own_ready, 3 * S + j + 1)
                        nc.scalar.activation(ZH[j][:], ZF[j], ACT.Copy).then_inc(own_high, 1)
                if u == 0 and attn:
                    exps(2, QB)
                    normalise()
                if mlp:
                    tanh(F)
                    high_h(F, 0, u == 0)
                if u > 0 and attn:
                    exps()
                    normalise()
                if mlp and u > 0:
                    tanh(F + 1)
                if attn:
                    probs_t()
                if mlp and u == 0:
                    tanh(F + 1)
                if mlp:
                    high_h(F + 1, 1, False)
                if u == SQ - 1 and attn:
                    if mlp:
                        wait(act, up_ready, NF * S + NF)
                    wait(act, x3_ready, SQ * it + SQ - 1)
                    high_x(k - (SQ - 1), 0, SQ - 1)
                if u == SQ - 1 and mlp:
                    wait(act, own_ready, 3 * S + 3)
                    nc.scalar.activation(ZH[2][:], ZF[0], ACT.Copy).then_inc(own_high, 1)
                if attn:
                    heads_t()
                if u == SQ - 1 and attn:
                    wait(act, x3_ready, SQ * it + SQ)
                    high_x(k, SQ - 1, 1)
                if u == SQ - 1 and mlp:
                    outputs_t()

            phase_b(step_b, act)

        @block.vector
        def _(dve):
            done = [0]

            def link(ins):
                done[0] += 1
                ins.then_inc(setup_done, 1)
                dve.wait_ge(setup_done, done[0])

            v = nc.vector
            dve.wait_ge(counts_started, 1)
            dve.wait_ge(rows_loaded, 32)
            link(v.tensor_scalar(ROWF[:], SUBT, float(T), cc(C_C32), ALU.mult, ALU.add))
            v.tensor_copy(WIDX[:], ROWF[:]).then_inc(subject_index, 1)
            dve.wait_ge(tables_loaded, 64)
            link(v.tensor_scalar(POS[:], KVT, cc(C_C32), None, ALU.add))
            link(v.tensor_tensor(ANG[:], POS[:].unsqueeze(2).broadcast_to([P, NQ, HALF]),
                                 cc(C_INV, HALF).unsqueeze(1).broadcast_to([P, NQ, HALF]), ALU.mult))
            magic = 1.5 * 2.0 ** 23
            c1, c2, c3 = two_pi_parts()
            v.tensor_scalar(TRG[:, 0], ANG[:], 1.0 / (2 * np.pi), 0.25, ALU.mult, ALU.add)
            link(v.tensor_scalar(TRG[:, 1], ANG[:], 1.0 / (2 * np.pi), None, ALU.mult))
            link(v.tensor_scalar(TRK[:], TRG[:], magic, None, ALU.add))
            link(v.tensor_scalar(TRG[:], TRK[:], -magic, None, ALU.add))
            for i in range(2):
                link(v.scalar_tensor_tensor(TRK[:, i], TRG[:, i], -c1, ANG[:], ALU.mult, ALU.add))
            trg, trk = (t[:].rearrange("p a n f -> p (a n f)") for t in (TRG, TRK))
            link(v.scalar_tensor_tensor(trk, trg, -c2, trk, ALU.mult, ALU.add))
            link(v.scalar_tensor_tensor(trk, trg, -c3, trk, ALU.mult, ALU.add))
            link(v.tensor_scalar(TRK[:, 0], TRK[:, 0], float(np.pi / 2), None, ALU.add))
            v.tensor_scalar(TRK[:], TRK[:], 3.1415925, -3.1415925, ALU.min, ALU.max)
            v.tensor_scalar(ONE[:, 0], SCL[:], 1.0, None, ALU.add)
            v.tensor_scalar(ONE[:, 1], SCL[:], -1.0, -1.0, ALU.mult, ALU.add).then_inc(angles_ready, 1)
            v.tensor_scalar(LMASK[:], SUBI[:], cc(C_N16), None, ALU.is_equal)
            v.tensor_scalar(SLOTI[:, 0:1], KVI[:], 4, None, ALU.logical_shift_right)
            v.tensor_scalar(SLOTI[:, 1:2], KVI[:], 15, None, ALU.bitwise_and)
            for bit in range(4):
                v.tensor_scalar(BITI[:, bit:bit + 1], KVI[:], bit, 1, ALU.logical_shift_right, ALU.bitwise_and)
            v.tensor_copy(TABF[:], TABI[:])
            link(v.tensor_scalar(THR[:], KVI[:], -1.0, float(WINDOW), ALU.mult, ALU.add))
            v.tensor_scalar(KVM[:], cc(C_IOTA, KEYS, B), THR[:, 0:1], NEG, ALU.is_lt, ALU.mult).then_inc(valid_ready, 1)
            link(v.tensor_copy(SLOTF[:], SLOTI[:]))
            v.tensor_copy(BITF[:], BITI[:])
            link(v.tensor_scalar(SJ[:], cc(C_IOTA, TWN, B), SLOTF[:, 0:1], float(-(WINDOW // BLOCK)), ALU.add, ALU.add))
            for j in range(TWN):
                link(v.scalar_tensor_tensor(TSCR[:, j % 2, :], cc(C_IOTA, NBLK, B), SJ[:, j:j + 1], TABF[:], ALU.is_equal, ALU.mult,
                                            accum_out=TW[:, j:j + 1]))
            link(v.tensor_scalar(TW16[:], TW[:], float(BLOCK), None, ALU.mult))
            link(v.tensor_tensor(KA[:], TW16[:].unsqueeze(2).broadcast_to([B, TWN, BLOCK]),
                                 cc(C_IOTA, BLOCK, B).unsqueeze(1).broadcast_to([B, TWN, BLOCK]), ALU.add))
            kaf = KA[:].rearrange("b j o -> b (j o)")
            for bit in (3, 2, 1, 0):
                by, width = 2 ** bit, KEYS + 2 ** bit - 1
                link(v.tensor_tensor(KDIF[:, 0:width], kaf[:, by:by + width], kaf[:, 0:width], ALU.subtract))
                link(v.scalar_tensor_tensor(kaf[:, 0:width], KDIF[:, 0:width], BITF[:, bit:bit + 1], kaf[:, 0:width], ALU.mult, ALU.add))
            keyt = kaf[:, 0:KEYS]
            v.tensor_tensor(K1E[:], keyt[:, P:KEYS].unsqueeze(1).broadcast_to([B, QB, T]),
                            cc(C_B4, QB, B).unsqueeze(2).broadcast_to([B, QB, T]), ALU.mult).then_inc(keys_ready, 1)
            rem = SLOTF[:, 1:2]
            last = TW16[:, TWN - WSLOT:TWN]
            v.tensor_copy(LHC[:, 0, 1:3], last[:, 1:3])
            v.tensor_scalar(LHC[:, 0, 0:1], last[:, 0:1], rem, None, ALU.add)
            v.tensor_scalar(LHC[:, 1, 0:2], last[:, 0:2], float(BLOCK - 1), None, ALU.add)
            v.tensor_scalar(LHC[:, 1, 2:3], last[:, 2:3], rem, -1.0, ALU.add, ALU.add)
            link(v.tensor_scalar(LHC[:, 2, :], last, -1.0, rem, ALU.mult, ALU.subtract))
            link(v.scalar_tensor_tensor(TSCR[:, 0, 0:WSLOT], cc(C_IOTA, WSLOT, B), float(BLOCK), LHC[:, 2, :], ALU.mult, ALU.add))
            link(v.tensor_scalar(LHC[:, 2, :], TSCR[:, 0, 0:WSLOT], cc(C_B32, 1, B), CBIG, ALU.add, ALU.add))
            v.tensor_tensor(LHCE[:].rearrange("b x i c -> b (x i) c"),
                            LHC[:].rearrange("b x i -> b (x i)").unsqueeze(2).broadcast_to([B, 3 * WSLOT, B]),
                            cc(C_ID, B, B).unsqueeze(1).broadcast_to([B, 3 * WSLOT, B]), ALU.mult).then_inc(intervals_ready, 1)
            dve.wait_ge(keys_spread, 4)
            dve.wait_ge(keys_zeroed, 1)
            v.tensor_copy(KEYS_[:, 0:NQ, 0:QB], PS[:, 7, 0:B].rearrange("p (n j) -> p n j", j=QB))
            v.tensor_copy(KEYS_[:, 0:NQ, QB], PS[:, 7, B:B + NQ])
            v.tensor_copy(WLHC[:, 0:2, :].rearrange("p x w -> p (x w)"), PS[:, 6, 0:2 * NW])
            v.tensor_copy(WLHC[:, 2, :], PS[:, 5, 0:NW]).then_inc(keys_kept, 1)
            dve.wait_ge(keys_kept, 1)
            for n in range(SQ):
                v.tensor_scalar(OIDX[n][:], KEYS_[:, n, 0:QB], 0.0, None, ALU.add).then_inc(old_index, 1)

            def blocks(n, i):
                wait(dve, xw0_ready, n - 1)
                wait(dve, x2_summed, n - 1)
                mask = cc(C_BLK, QB).unsqueeze(2).broadcast_to([P, QB, T])
                w = WL[:, bass.ds(n, 1), :].rearrange("p o c -> p (o c)")
                wait(dve, blocks_ready, n)
                v.tensor_tensor(BDT[:], w[:, T:2 * T].unsqueeze(1).broadcast_to([P, QB, T]), mask, ALU.mult).then_inc(w1_blocks, 1)
                v.tensor_tensor(BD0[i][:], w[:, 0:T].unsqueeze(1).broadcast_to([P, QB, T]), mask, ALU.mult)
                wait(dve, w1_blocks, n + 1)
                v.tensor_tensor(BD1[i][:], BDT[:], cc(C_ID, P).rearrange("p (j c) -> p j c", j=QB), ALU.add).then_inc(blocks_ready, 1)

            def step_a(it, u):
                k = it * SQ + u
                if has(k):
                    blocks(k, u % 2)
                n, i = k - 1, (u - 1) % 2
                if has(n):
                    wait(dve, xw0_ready, n + 1)
                    wait(dve, x2_summed, n - 1)
                    v.scalar_tensor_tensor(X1[i][:], PS[:, i, 0:D], WL[:, bass.ds(n, 1), 2 * T:2 * T + 1].rearrange("p o c -> p (o c)"),
                                           X[:, bass.ds(n, 1), :].rearrange("p o d -> p (o d)"), ALU.add, ALU.add).then_inc(x1_ready, 1)
                n, s = k - 4, u
                if has(n):
                    wait(dve, roots_ready, n + 1)
                    wait(dve, k_ready, n)
                    v.reciprocal(SS[s][:, 2, :], SS[s][:, 1, :]).then_inc(inverses_ready, 1)
                n, i, s = k - 3, (u - 3) % 2, (u - 3) % SQ
                if has(n):
                    wait(dve, squares_ready, n + 1)
                    v.reduce_sum(SS[s][:, 0, :], SQR[i][:], AX_X).then_inc(square_sums, 1)
                    wait(dve, v_ready, n + 1)
                    wait(dve, rotated, n - 1)
                    qk = PS[:, 4 + i, 0:12 * HD].rearrange("p (h d) -> p h d", h=12)
                    tc = TC[:, bass.ds(n, 1), :, :].rearrange("p o a d -> p (o a) d")
                    ts = TS[:, bass.ds(n, 1), :, :].rearrange("p o a d -> p (o a) d")
                    for a, lo, hi in ((0, 0, 8), (1, 8, 12)):
                        m = hi - lo
                        v.tensor_tensor(RA[i][:, lo:hi, :], qk[:, lo:hi, :], tc[:, a:a + 1, :].broadcast_to([P, m, HD]), ALU.mult)
                        for h in range(2):
                            hs, other = slice(HALF * h, HALF * h + HALF), slice(HALF * (1 - h), HALF * (1 - h) + HALF)
                            last = v.tensor_tensor(RB[i][:, lo:hi, hs], qk[:, lo:hi, other], ts[:, a:a + 1, hs].broadcast_to([P, m, HALF]), ALU.mult)
                    last.then_inc(rope_parts, 1)
                n = k - 4
                if has(n):
                    wait(dve, rotated, n + 1)
                    wait(dve, inverses_ready, n + 1)
                    wait(dve, new_stored[u], 16 * (it - 1))
                    v.tensor_tensor(KVN[u][:, 0:P].rearrange("p (h d) -> p h d", h=G), RS_[u % 2][:, 8:12, :],
                                    SS[u][:, 2, 8:12].unsqueeze(2).broadcast_to([P, G, HD]), ALU.mult).then_inc(k_ready, 1)

            dve.wait_ge(subject_rows[0], 16 * SQ)
            dve.wait_ge(x_first_loaded, 16)
            for u in range(SQ):
                if u == SQ - 1:
                    dve.wait_ge(rope_ready, 1)
                step_a(0, u)
            dve.wait_ge(subject_rows[1], 16 * (NQ - SQ))
            dve.wait_ge(x_rest_loaded, 16)
            with dve.Fori(1, NQ // SQ) as it:
                for u in range(SQ):
                    step_a(it, u)
            def match(it, u):
                match_low(it, u)
                match_high(it, u)

            def match_low(it, u):
                k = it * SQ + u
                wait(dve, new_index, k)
                for j in range(QB + 1):
                    key = KEYS_[:, bass.ds(k, 1), j:j + 1].rearrange("p o c -> p (o c)")
                    v.scalar_tensor_tensor(U[:, j, :], WLHC[:, 0, :], key, WLHC[:, 2, :], ALU.is_le, ALU.mult).then_inc(low_tested, 1)
                if not isinstance(it, int) or it > 0:
                    wait(dve, old_gathered[u], it * 16 * QB)
                    v.tensor_scalar(OIDX[u][:], KEYS_[:, bass.ds(k, 1), 0:QB].rearrange("p o c -> p (o c)"), 0.0, None, ALU.add).then_inc(old_index, 1)

            def match_high(it, u):
                k = it * SQ + u
                for j in range(QB + 1):
                    key = KEYS_[:, bass.ds(k, 1), j:j + 1].rearrange("p o c -> p (o c)")
                    wait(dve, low_tested, (QB + 1) * k + j + 1)
                    last = v.scalar_tensor_tensor(U[:, j, :], WLHC[:, 1, :], key, U[:, j, :], ALU.is_ge, ALU.mult)
                last.then_inc(high_tested, 1)
                wait(dve, high_tested, k + 1)
                v.tensor_reduce(CM[:, 0, :], U[:], AX_X, ALU.max).then_inc(code_found, 1)
                wait(dve, code_found, k + 1)
                v.tensor_scalar(CM[:, 1, :], CM[:, 0, :], 0.0, 4.0 * CBIG, ALU.is_equal, ALU.mult)
                v.tensor_tensor(CM[:, 2, :], CM[:, 0, :], KEYS_[:, bass.ds(k, 1), :].rearrange("p o c -> p (o c)"), ALU.add).then_inc(token_found, 1)
                wait(dve, token_found, k + 1)
                wait(dve, new_gathered[u % 2], uses(it - 1, u, QB + 1))
                v.scalar_tensor_tensor(NIDX[u][:], CM[:, 2, :], -CBIG, CM[:, 1, :], ALU.add, ALU.add).then_inc(new_index, 1)

            for u in range(SQ):
                if u == SQ - 1:
                    match_low(0, 0)
                step_a(NQ // SQ, u)
            match_high(0, 0)
            match(0, 1)

            def gated(F):
                wait(dve, tanh_ready, F + 1)
                v.scalar_tensor_tensor(GA, TH, 1.0, PS[:, 0, :], ALU.add, ALU.mult).then_inc(gated_ready, 1)
                wait(dve, gated_ready, F + 1)
                wait(dve, up_ready, F + 1)
                wait(dve, h_high, F)
                v.scalar_tensor_tensor(HF[:], PS[:, 1, :], 0.5, GA, ALU.mult, ALU.mult).then_inc(h_ready, 1)

            def rest_h(F, f, first):
                wait(dve, h_high, F + 1)
                if not first:
                    wait(dve, down_added, F - 1)
                v.tensor_tensor(HR[f % 2][:], HF[:], HH[f % 2][:].bitcast(F32), ALU.subtract).then_inc(h_rest, 1)

            def own_adapter(S, j, bank, z):
                wait(dve, own_high, 3 * S + (2 if j == 2 else 0))
                own = LMASK[:, bass.ds(S * QB * SQ, QB * SQ)].unsqueeze(2).broadcast_to([P, QB * SQ, T])
                v.tensor_tensor(z.rearrange("p (b t) -> p b t", t=T), PS[:, bank, :].rearrange("p (b t) -> p b t", t=T),
                                own, ALU.mult).then_inc(own_ready, 1)

            def rest_z(S, j, z):
                wait(dve, own_high, 3 * S + j + 1)
                v.tensor_tensor(ZR[j][:], z, ZH[j][:].bitcast(F32), ALU.subtract).then_inc(own_rest, 1)

            def rest_x(k, at, n):
                cols = slice(P * at, P * (at + n))
                v.tensor_tensor(XR[:, :, cols], XT[:, :, bass.ds(k * P, P * n)], XH[:, :, cols].bitcast(F32), ALU.subtract).then_inc(x3_rest, 1)

            def add_attention(k):
                wait(dve, attn_ready, k + 1)
                xq = XT[:, :, bass.ds(k * P, P)]
                v.tensor_tensor(xq, ring[:, 2, 0:2 * P].rearrange("p (h t) -> p h t", h=2), xq, ALU.add).then_inc(x3_ready, 1)

            def step_b(it, u, attn, mlp):
                k = it * SQ + u
                S = it - 1
                F = S * NF + 2 * u

                def maxima(first=0, last=QB):
                    for b in range(first, last):
                        wait(dve, scores_ready, QB * k + b + 1)
                        if b == 0:
                            wait(dve, exps_ready, 2 * QB * k)
                        v.reduce_max(MX[:, b, :], ring[:, b % 3, 0:2 * KEYS].rearrange("p (g r) -> p g r", g=2), AX_X).then_inc(maxima_found, 1)
                        wait(dve, maxima_found, QB * k + b + 1)
                        v.tensor_scalar(NB[:, b, :], MX[:, b, :], -SCALE, None, ALU.mult).then_inc(bias_ready, 1)

                def normalise():
                    wait(dve, exps_ready, 2 * QB * (k + 1))
                    v.reciprocal(RINV[:].rearrange("p b g -> p (b g)"), RSUM[:].rearrange("p b g -> p (b g)")).then_inc(sums_inverted, 1)
                    wait(dve, sums_inverted, k + 1)
                    wait(dve, probs_turned, 3 * k)
                    for b in range(2):
                        for gp in range(2):
                            v.tensor_scalar(PE_[:, b, gp, 0:P], PE_[:, b, gp, 0:P], RINV[:, b, gp:gp + 1], None, ALU.mult)
                    v.tensor_tensor(PR1[:], PE_[:, :, :, P:KEYS].rearrange("p b g r -> p g b r"),
                                    RINV[:].rearrange("p b g -> p g b").unsqueeze(3).broadcast_to([P, 2, QB, T]), ALU.mult).then_inc(probs_ready_dve, 1)

                if mlp and u == 0:
                    wait(dve, low_rank_ready, 2 * S + 1)
                    own_adapter(S, 0, 4, ZF[0])
                if u == 0 and attn:
                    maxima(0, 2)
                if mlp and u == 0:
                    wait(dve, low_rank_ready, 2 * S + 2)
                    own_adapter(S, 1, 2, ZF[1])
                if u == 0 and attn:
                    maxima(2, QB)
                if mlp and u == 0:
                    rest_z(S, 0, ZF[0])
                    rest_z(S, 1, ZF[1])
                if u == 0 and attn:
                    normalise()
                if mlp:
                    gated(F)
                if u > 0 and attn:
                    add_attention(k - 1)
                if mlp:
                    rest_h(F, 0, u == 0)
                if u > 0 and attn:
                    maxima()
                    normalise()
                if attn and not mlp and u < SQ - 1:
                    match_low(it + (u + 2) // SQ, (u + 2) % SQ)
                if mlp and u > 0:
                    gated(F + 1)
                if attn:
                    wait(dve, heads_ready, k)
                    wait(dve, probs_turned, 3 * k + 3)
                    v.tensor_copy(PT1[:].rearrange("p g q -> p (g q)"), ring[:, 0, 0:2 * P]).then_inc(probs_taken_dve, 1)
                if mlp and u == 0:
                    gated(F + 1)
                if mlp:
                    rest_h(F + 1, 1, False)
                if u == SQ - 1 and attn:
                    wait(dve, x3_high, 2 * it + 1)
                    rest_x(k - (SQ - 1), 0, SQ - 1)
                    match_low(it + 1, 1)
                if u == SQ - 1 and mlp:
                    wait(dve, down_added, NF * S + NF)
                    own_adapter(S, 2, 4, ZF[0])
                    rest_z(S, 2, ZF[0])
                if u == SQ - 1 and attn:
                    add_attention(k)
                if u == SQ - 1 and mlp:
                    wait(dve, out_ready, S + 1)
                    wait(dve, out_turned, 2 * S)
                    for j in range(2):
                        half = slice(2 * P * j, 2 * P * j + 2 * P)
                        v.tensor_tensor(X4[:, :, half], PS[:, 2:4, half], XT[:, :, bass.ds(S * ST + 2 * P * j, 2 * P)], ALU.add).then_inc(x4_ready, 1)
                if u == SQ - 1 and attn:
                    wait(dve, x3_high, 2 * it + 2)
                    rest_x(k, SQ - 1, 1)
                if attn and mlp and u < SQ - 1:
                    match_low(it + (u + 2) // SQ, (u + 2) % SQ)
                if attn:
                    match_high(it + (u + 2) // SQ, (u + 2) % SQ)

            phase_b(step_b, dve)

        @block.tensor
        def _(pe):
            mm = nc.tensor.matmul
            ident = cc(C_ID, P)

            def tr(o, i):
                return nc.tensor.transpose(o, i, ident[0:i.shape[0], 0:i.shape[0]])

            def mm3(o, at, high, rest, start, stop):
                wh, wr = WH[:, at:at + P], WR[:, at:at + P]
                mm(o, wh, high, start=start, stop=False)
                mm(o, wh, rest, start=False, stop=False)
                return mm(o, wr, high, start=False, stop=stop)

            pe.wait_ge(counts_started, 1)
            pe.wait_ge(rows_loaded, 32)
            keyt = KA[:].rearrange("b j o -> b (j o)")
            pe.wait_ge(keys_ready, 1)
            tr(PS[:, 7, 0:B], keyt[:, 0:P]).then_inc(keys_spread, 1)
            mm(PS[:, 7, B:B + NQ], K1E[:].rearrange("b j t -> b (j t)"), cc(C_Q16, NQ, B), start=True, stop=True).then_inc(keys_spread, 1)
            pe.wait_ge(intervals_ready, 1)
            e = LHCE[:].rearrange("b x i c -> b (x i c)")
            mm(PS[:, 6, 0:2 * NW], cc(C_ONE, P, B), e[:, 0:2 * NW], start=True, stop=True).then_inc(keys_spread, 1)
            mm(PS[:, 5, 0:NW], cc(C_ONE, P, B), e[:, 2 * NW:3 * NW], start=True, stop=True).then_inc(keys_spread, 1)

            pe.wait_ge(x_first_loaded, 16)
            pe.wait_ge(wqkv_loaded, 16)
            pe.wait_ge(keys_kept, 1)

            def step_a(it, u):
                k = it * SQ + u
                if has(k):
                    wait(pe, blocks_ready, k + 1)
                    wait(pe, x1_ready, k - 1)
                    mm(PS[:, u % 2, 0:D], BD0[u % 2][:].rearrange("p j c -> p (j c)"), X[:, bass.ds(k, 1), :], start=True, stop=True).then_inc(xw0_ready, 1)
                n, i = k - 1, (u - 1) % 2
                if has(n):
                    wait(pe, x1_ready, n + 1)
                    wait(pe, x2_kept, n - 1)
                    for h in range(2):
                        last = mm(PS[:, 2 + i, P * h:P * h + P], X1[i][:, P * h:P * h + P], BD1[i][:].rearrange("p j c -> p (j c)"), start=True, stop=True)
                    last.then_inc(x2_summed, 1)
                n, i = k - 2, u % 2
                if has(n):
                    wait(pe, x2_kept, n + 1)
                    wait(pe, rope_parts, n - 1)
                    wait(pe, v_ready, n - 1)
                    for h in range(2):
                        last = mm(PS[:, 4 + i, :], X2S[i][:, h, :], WQKV[:, h, :], start=h == 0, stop=h == 1)
                    last.then_inc(qkv_ready, 1)
                n = k - 4
                if has(n):
                    wait(pe, q_ready, n + 1)
                    wait(pe, qt_kept, n)
                    for h in range(2):
                        last = tr(PS[:, 6 + u % 2, P * h:P * h + P], QR[u][:, G * h:G * h + G, :].rearrange("p h d -> p (h d)"))
                    last.then_inc(qt_summed, 1)

            phase_a(step_a, NQ + 3, pe)
            wait(pe, qt_kept, NQ)
            pe.wait_ge(rope_parts, NQ)
            wait(pe, v_ready, NQ)
            pe.wait_ge(x2_kept, NQ)
            pe.wait_ge(mask_loaded, 48)
            pe.wait_ge(wo_loaded, 16)
            pe.wait_ge(rest_split, NQ)

            def low_rank(S):
                wait(pe, x3_rest, 2 * (S + 1))
                wait(pe, own_ready, 3 * S)
                wait(pe, x4_ready, 2 * S)
                for bank, at in ((4, W_AG), (2, W_AU)):
                    for h in range(2):
                        last = mm3(PS[:, bank, :], at + P * h, XH[:, h, :], XR[:, h, :], h == 0, h == 1)
                    last.then_inc(low_rank_ready, 1)

            def up_base(S, f):
                F = S * NF + f
                wait(pe, gated_ready, F)
                if f == 0:
                    wait(pe, out_taken, 2 * S)
                for h in range(2):
                    mm3(PS[:, 0, :], W_G + FF * h + P * f, XH[:, h, :], XR[:, h, :], h == 0, False)
                wait(pe, h_ready, F)
                for h in range(2):
                    mm3(PS[:, 1, :], W_U + FF * h + P * f, XH[:, h, :], XR[:, h, :], h == 0, False)

            def up_low(S, f):
                if f == 0:
                    wait(pe, own_rest, 3 * S + 2)
                mm3(PS[:, 0, :], W_BG + P * f, ZH[0][:], ZR[0][:], False, True).then_inc(gate_ready, 1)
                mm3(PS[:, 1, :], W_BU + P * f, ZH[1][:], ZR[1][:], False, True).then_inc(up_ready, 1)

            def up(S, f):
                F = S * NF + f
                wait(pe, gated_ready, F)
                for h in range(2):
                    mm3(PS[:, 0, :], W_G + FF * h + P * f, XH[:, h, :], XR[:, h, :], h == 0, False)
                mm3(PS[:, 0, :], W_BG + P * f, ZH[0][:], ZR[0][:], False, True).then_inc(gate_ready, 1)
                wait(pe, h_ready, F)
                for h in range(2):
                    mm3(PS[:, 1, :], W_U + FF * h + P * f, XH[:, h, :], XR[:, h, :], h == 0, False)
                mm3(PS[:, 1, :], W_BU + P * f, ZH[1][:], ZR[1][:], False, True).then_inc(up_ready, 1)

            def down(S, f):
                wait(pe, h_rest, S * NF + f + 1)
                if f == 0:
                    wait(pe, own_ready, 3 * S + 2)
                for h in range(2):
                    mm3(PS[:, 2 + h, :], W_D + D * f + P * h, HH[f % 2][:], HR[f % 2][:], f == 0, False)
                mm3(PS[:, 4, :], W_AD + P * f, HH[f % 2][:], HR[f % 2][:], f == 0, f == NF - 1).then_inc(down_added, 1)

            def output_proj(k):
                wait(pe, heads_taken, k + 1)
                for h in range(2):
                    for hl in range(2):
                        last = mm(ring[:, 2, P * h:P * h + P], WO[:, hl, P * h:P * h + P], OT[:, hl, :, :].rearrange("p b t -> p (b t)"),
                                  start=hl == 0, stop=hl == 1)
                last.then_inc(attn_ready, 1)

            def step_b(it, u, attn, mlp):
                k = it * SQ + u
                S = it - 1

                def keys_t():
                    wait(pe, new_gathered[u % 2], uses(it, u, QB + 1))
                    for b in range(QB):
                        last = tr(ring[:, 0, P * b:P * b + P], KV0[u][:, b, 0:P])
                    last.then_inc(keys_turned, 1)
                    tr(ring[:, 1, 0:P], KV1[u % 2][:, 0:P]).then_inc(keys_turned, 1)

                def scores():
                    wait(pe, keys_taken, k + 1)
                    wait(pe, q_spread, G * (k + 1))
                    wait(pe, valid_loaded[u % 2], uses(it, u, 1))
                    for b in range(QB):
                        if b == 2:
                            wait(pe, x3_ready, k)
                        if b == 3:
                            wait(pe, exps_ready, 2 * QB * k + 2)
                        mm(ring[:, b % 3, 0:2 * KEYS], PICK[:], MASK[u % 2][:, b, :].unsqueeze(1).broadcast_to([T + 1, 2, KEYS]), start=True, stop=False)
                        for gp in range(2):
                            last = mm(ring[:, b % 3, KEYS * gp:KEYS * gp + KEYS], QBD[u % 2][:, b, gp, :], KT[:, b, :], start=False, stop=gp == 1)
                        last.then_inc(scores_ready, 1)

                def probs_t():
                    wait(pe, probs_ready_dve, k + 1)
                    for b in range(QB):
                        if b == 2:
                            wait(pe, probs_ready_act, k + 1)
                        for gp in range(2):
                            j = 2 * b + gp
                            last = tr(ring[:, 1 + j // 4, P * (j % 4):P * (j % 4) + P], PE_[:, b, gp, 0:P])
                        if b % 2:
                            last.then_inc(probs_turned, 1)
                    for gp in range(2):
                        last = tr(ring[:, 0, P * gp:P * gp + P], PR1[:, gp, :, :].rearrange("p b r -> p (b r)"))
                    last.then_inc(probs_turned, 1)

                def weigh_v():
                    wait(pe, probs_taken_dve, k + 1)
                    wait(pe, probs_taken_act, 2 * k + 2)
                    wait(pe, v_parted, k + 1)
                    for b in range(QB):
                        for start in (True, False):
                            for g in range(G):
                                rows, qs = slice(HD * g, HD * g + HD), slice(64 * (g % 2), 64 * (g % 2) + 64)
                                o = ring[rows, 2, 64 * b:64 * b + 64]
                                if start:
                                    mm(o, KV0[u][:, b, P + HD * g:P + HD * g + HD], PT0[:, b, g // 2, qs], start=True, stop=False)
                                else:
                                    last = mm(o, V1M[u % 2][:, b, HD * g:HD * g + HD], PT1[:, g // 2, qs], start=False, stop=True)
                    last.then_inc(heads_ready, 1)

                if attn:
                    keys_t()
                if u == 0:
                    if mlp:
                        low_rank(S)
                    if attn:
                        scores()
                    if mlp:
                        up_base(S, 0)
                        up_low(S, 0)
                    if attn:
                        probs_t()
                    if mlp:
                        up(S, 1)
                    if attn:
                        weigh_v()
                    if mlp:
                        down(S, 0)
                    return
                if mlp:
                    up(S, 2 * u)
                if attn:
                    output_proj(k - 1)
                if mlp:
                    down(S, 2 * u - 1)
                if attn:
                    scores()
                if mlp:
                    up(S, 2 * u + 1)
                if attn:
                    probs_t()
                if mlp:
                    down(S, 2 * u)
                if u == SQ - 1 and mlp:
                    down(S, NF - 1)
                if attn:
                    weigh_v()
                if u == SQ - 1 and attn:
                    output_proj(k)
                if u == SQ - 1 and mlp:
                    wait(pe, own_rest, 3 * S + 3)
                    for h in range(2):
                        last = mm3(PS[:, 2 + h, :], W_BD + P * h, ZH[2][:], ZR[2][:], False, True)
                    last.then_inc(out_ready, 1)
                    for j in range(2):
                        wait(pe, x4_ready, 2 * S + j + 1)
                        for n in range(2):
                            for h in range(2):
                                last = tr(PS[:, j, D * n + P * h:D * n + P * h + P], X4[:, h, P * (2 * j + n):P * (2 * j + n) + P])
                        last.then_inc(out_turned, 1)

            phase_b(step_b, pe)


def kernel(x, itok_B_0_7, fside_8xS_0, itok_Bx257_0_4111, itok_B_37_3939, L0_cond_weights, L1_cond_weights,
           L2_cond_Wq, L2_cond_Wk, L2_cond_Wv, L2_cond_Wo, L2_cond_q_norm_scale, L2_cond_k_norm_scale,
           L2_cond_k_blocks, L2_cond_v_blocks, L3_cond_Wg, L3_cond_Wu, L3_cond_Wd, L3_cond_Ag, L3_cond_Bg,
           L3_cond_Au, L3_cond_Bu, L3_cond_Ad, L3_cond_Bd):
    import ml_dtypes
    import concourse.bacc as bacc
    from concourse.bass_utils import run_bass_kernel_spmd

    def lay(a, *shape):
        return np.ascontiguousarray(np.asarray(a).reshape(shape))

    def flip(a, *order):
        return np.ascontiguousarray(np.transpose(np.asarray(a), order))

    wq = flip(lay(L2_cond_Wq, G, 2, HD, D), 3, 1, 0, 2).reshape(D, P * 2)
    wk, wv = flip(L2_cond_Wk, 1, 0), flip(L2_cond_Wv, 1, 0)
    wqkv = flip(np.concatenate([wq, wk, wv], 1).reshape(2, P, 4 * P), 1, 0, 2)
    wo = flip(lay(L2_cond_Wo, D, G, 2, HD), 1, 3, 2, 0).reshape(P, 2, D)

    def rows(w, n):
        return flip(lay(w, n, P, -1), 1, 0, 2)

    def low(a, n):
        return rows(flip(a, 1, 0, 2).reshape(n * P, P), n)

    kvpool = np.concatenate([flip(L2_cond_k_blocks, 0, 2, 1, 3).reshape(NPHYS * BLOCK, P),
                             flip(L2_cond_v_blocks, 0, 2, 1, 3).reshape(NPHYS * BLOCK, P)], 1)
    wl = np.concatenate([lay(L0_cond_weights, NS * T, T), lay(L1_cond_weights, NS * T, T), lay(fside_8xS_0, NS * T, 1)], 1)
    wmlp = np.concatenate([lay(w, P, -1) for w in (
        rows(L3_cond_Wg, 2), rows(L3_cond_Wu, 2), rows(L3_cond_Wd, NF), low(L3_cond_Ad, NF), low(L3_cond_Ag, 2),
        low(L3_cond_Au, 2), L3_cond_Bg, L3_cond_Bu, L3_cond_Bd)], 1)
    perpart = np.concatenate([np.repeat(flip(lay(a, NQ, QB), 1, 0), T, 0) for a in (itok_B_0_7, itok_B_37_3939)], 1)
    window, pick = mask_constants(ml_dtypes.bfloat16)
    arrays = {
        "x": lay(x, NTOK, D), "wl": wl, "wqkv": wqkv, "wo": wo, "wmlp": wmlp,
        "scales": np.concatenate([np.asarray(L2_cond_q_norm_scale), np.asarray(L2_cond_k_norm_scale)]),
        "kvpool": kvpool, "subj": lay(itok_B_0_7, B), "kvlen": lay(itok_B_37_3939, B), "perpart": perpart,
        "table": lay(itok_Bx257_0_4111, B, NBLK),
        "consts": constants(), "window": window, "pick": pick,
    }
    nc = bacc.Bacc("TRN2", target_bir_lowering=False, num_devices=1)
    arrays = {f"in_{n}": a for n, a in arrays.items()}
    args = [nc.dram_tensor(n, a.shape, mybir.dt.from_np(a.dtype), kind="ExternalInput").ap() for n, a in arrays.items()]
    out = nc.dram_tensor("out_0", (NTOK, D), F32, kind="ExternalOutput").ap()
    knew = nc.dram_tensor("k_new", (NTOK, KV), F32).ap()
    valid = nc.dram_tensor("key_valid", (B, KEYS), BF16).ap()
    build(nc, *args, out, knew, valid)
    r = run_bass_kernel_spmd(nc, [arrays], core_ids=[0])
    return r.results[0]["out_0"].reshape(B, T, D)
```
